# Optimizing a Trainium2 kernel written in Bass

```python
import numpy as np
import jax
import jax.numpy as jnp

def _softmax(x, axis=-1):
    return jax.nn.softmax(x, axis=axis)

def _gelu(x):
    return jax.nn.gelu(x, approximate=True)

def _silu(x):
    return jax.nn.silu(x)

def _sigmoid(x):
    return jax.nn.sigmoid(x)

def _layernorm(x, axis=-1, eps=1e-05):
    m = jnp.mean(x, axis=axis, keepdims=True)
    v = jnp.var(x, axis=axis, keepdims=True)
    return (x - m) / jnp.sqrt(v + eps)

def _scatter_add(tgt, idx, src, axis=0):
    return tgt.at[idx].add(src)

def _segment_sum(src, seg, n):
    return jax.ops.segment_sum(src, seg, n)
kernel_name = 'mk_gnn_preln_d4_gnn_r8_9490ce'

def setup_inputs(seed: int=0):
    np.random.seed(seed)
    _w = jnp.asarray

    def _rec_inputs():
        import jax
        import jax.numpy as jnp
        _gk = jax.random.key(seed)
        x = -0.000202 + 1 * jax.random.normal(jax.random.fold_in(_gk, 1), (12500, 64), jnp.float32)
        src = jax.random.randint(jax.random.fold_in(_gk, 2), (200000,), 0, 12500, jnp.int32)
        dst = jnp.minimum((12500 * jax.random.uniform(jax.random.fold_in(_gk, 3), (200000,)) ** 2.0).astype(jnp.int32), 99999)
        _o = jnp.argsort(dst, stable=True)
        src = src[_o]
        dst = dst[_o]
        edge_attr_64 = -6.74381e-05 + 0.999835 * jax.random.normal(jax.random.fold_in(_gk, 12), (200000, 64), jnp.float32)
        edge_type_10 = jax.random.randint(jax.random.fold_in(_gk, 14), (200000,), 0, 10, jnp.int32)
        edge_type_8 = jax.random.randint(jax.random.fold_in(_gk, 15), (200000,), 0, 8, jnp.int32)
        return (x, src, dst, edge_attr_64, edge_type_10, edge_type_8)
    x, src, dst, edge_attr_64, edge_type_10, edge_type_8 = _rec_inputs()

    def _L0_gnn_setup():
        import jax, jax.numpy as jnp
        import numpy as np
        N_NODES = 12500
        N_EDGES = 200000
        IN_FEAT = 64
        HIDDEN = 64

        def _sage_conv(h, src, dst, W_l, b, W_r):
            n = h.shape[0]
            msg = h[src]
            agg = jax.ops.segment_sum(msg, dst, num_segments=n)
            cnt = jax.ops.segment_sum(jnp.ones((src.shape[0],), h.dtype), dst, num_segments=n)
            mean = agg / jnp.maximum(cnt, 1.0)[:, None]
            return mean @ W_l.T + b + h @ W_r.T
        key = jax.random.key(seed)
        ks = jax.random.split(key, 8)
        s = 0.05
        x = jax.random.normal(ks[0], (N_NODES, IN_FEAT), dtype=jnp.float32)
        edge_index = jax.random.randint(ks[1], (2, N_EDGES), 0, N_NODES, dtype=jnp.int64)
        return {'x': x, 'edge_index': edge_index, 'W_l1': jax.random.normal(ks[2], (HIDDEN, IN_FEAT), dtype=jnp.float32) * s, 'b1': jnp.zeros((HIDDEN,), dtype=jnp.float32), 'W_r1': jax.random.normal(ks[3], (HIDDEN, IN_FEAT), dtype=jnp.float32) * s, 'W_l2': jax.random.normal(ks[4], (HIDDEN, HIDDEN), dtype=jnp.float32) * s, 'b2': jnp.zeros((HIDDEN,), dtype=jnp.float32), 'W_r2': jax.random.normal(ks[5], (HIDDEN, HIDDEN), dtype=jnp.float32) * s}
    _L0_gnn_all = _L0_gnn_setup()
    _L0_gnn_in = {k: v for k, v in _L0_gnn_all.items() if k in ('W_l1', 'b1', 'W_r1', 'W_l2', 'b2', 'W_r2')}
    del _L0_gnn_all

    def _L1_gnn_setup():
        import jax, jax.numpy as jnp
        import numpy as np
        NUM_NODES = 12500
        EMBED_DIM = 64
        NUM_LAYERS = 3
        NUM_EDGES = 400000

        def _lightgcn_embedding(emb, edge_index):
            n = emb.shape[0]
            src, dst = (edge_index[0], edge_index[1])
            deg = jax.ops.segment_sum(jnp.ones(src.shape[0], dtype=emb.dtype), dst, num_segments=n)
            deg_inv_sqrt = jnp.where(deg > 0, jax.lax.rsqrt(jnp.maximum(deg, 1.0)), 0.0)
            w = deg_inv_sqrt[src] * deg_inv_sqrt[dst]
            x = emb
            out = emb
            for _ in range(NUM_LAYERS):
                x = jax.ops.segment_sum(w[:, None] * x[src], dst, num_segments=n)
                out = out + x
            return out / (NUM_LAYERS + 1)
        key = jax.random.key(seed)
        k_emb, k_edge = jax.random.split(key)
        emb = jax.random.normal(k_emb, (NUM_NODES, EMBED_DIM), dtype=jnp.float32) * 0.1
        edge_index = jax.random.randint(k_edge, (2, NUM_EDGES), 0, NUM_NODES, dtype=jnp.int64)
        return {'emb': emb, 'edge_index': edge_index}
    _L1_gnn_all = _L1_gnn_setup()
    _L1_gnn_in = {k: v for k, v in _L1_gnn_all.items() if k in ()}
    del _L1_gnn_all

    def _L2_gnn_setup():
        import jax, jax.numpy as jnp
        import numpy as np
        N_NODES = 12500
        N_EDGES = 160000
        HID = 64
        MSG = 64
        N_ETYPE = 8

        def _ggnn_forward(h, edge_matrix, w_ih, w_hh, b_ih, b_hh, edge_src, edge_dst, edge_type):
            N, H = h.shape
            T = edge_matrix.shape[0]
            M = edge_matrix.shape[1] // H
            A = edge_matrix.reshape(T, M, H)
            Ht = jnp.einsum('tmh,nh->tnm', A, h)
            msg = Ht[edge_type, edge_src]
            m_agg = jax.ops.segment_sum(msg, edge_dst, num_segments=N)
            gi = m_agg @ w_ih.T + b_ih
            gh = h @ w_hh.T + b_hh
            i_r, i_z, i_n = (gi[:, :H], gi[:, H:2 * H], gi[:, 2 * H:])
            h_r, h_z, h_n = (gh[:, :H], gh[:, H:2 * H], gh[:, 2 * H:])
            r = jax.nn.sigmoid(i_r + h_r)
            z = jax.nn.sigmoid(i_z + h_z)
            n = jnp.tanh(i_n + r * h_n)
            return (1.0 - z) * n + z * h
        key = jax.random.key(seed)
        ks = jax.random.split(key, 9)
        s = 1.0 / np.sqrt(HID)
        return {'h': jax.random.normal(ks[0], (N_NODES, HID), jnp.float32) * s, 'edge_matrix': jax.random.normal(ks[1], (N_ETYPE, MSG * HID), jnp.float32) * s, 'w_ih': jax.random.normal(ks[2], (3 * HID, MSG), jnp.float32) * s, 'w_hh': jax.random.normal(ks[3], (3 * HID, HID), jnp.float32) * s, 'b_ih': jax.random.normal(ks[4], (3 * HID,), jnp.float32) * s, 'b_hh': jax.random.normal(ks[5], (3 * HID,), jnp.float32) * s, 'edge_src': jax.random.randint(ks[6], (N_EDGES,), 0, N_NODES, jnp.int32), 'edge_dst': jax.random.randint(ks[7], (N_EDGES,), 0, N_NODES, jnp.int32), 'edge_type': jax.random.randint(ks[8], (N_ETYPE if False else N_EDGES,), 0, N_ETYPE, jnp.int32)}
    _L2_gnn_all = _L2_gnn_setup()
    _L2_gnn_in = {k: v for k, v in _L2_gnn_all.items() if k in ('edge_matrix', 'w_ih', 'w_hh', 'b_ih', 'b_hh')}
    del _L2_gnn_all

    def _L3_gnn_setup():
        import jax, jax.numpy as jnp
        import numpy as np
        NEG_SLOPE = 0.01
        N_NODES = 12500
        N_EDGES = 156250
        N_REL = 10
        D = 64
        key = jax.random.key(seed)
        ks = jax.random.split(key, 8)
        return {'nfeat': jax.random.normal(ks[0], (N_NODES, D), dtype=jnp.float32), 'efeat': jax.random.normal(ks[1], (N_EDGES, D), dtype=jnp.float32), 'relation_weight': jax.random.normal(ks[2], (N_REL, D, D), dtype=jnp.float32) * (1.0 / np.sqrt(D)), 'res_fc_w': jax.random.normal(ks[3], (D, D), dtype=jnp.float32) * (1.0 / np.sqrt(D)), 'res_fc2_w': jax.random.normal(ks[4], (D, D), dtype=jnp.float32) * (1.0 / np.sqrt(D)), 'src': jax.random.randint(ks[5], (N_EDGES,), 0, N_NODES, dtype=jnp.int32), 'dst': jnp.sort(jax.random.randint(ks[6], (N_EDGES,), 0, N_NODES, dtype=jnp.int32)), 'etype': jax.random.randint(ks[7], (N_EDGES,), 0, N_REL, dtype=jnp.int32)}
    _L3_gnn_all = _L3_gnn_setup()
    _L3_gnn_in = {k: v for k, v in _L3_gnn_all.items() if k in ('relation_weight', 'res_fc_w', 'res_fc2_w')}
    del _L3_gnn_all
    return {'x': x, 'src': src, 'dst': dst, 'edge_attr_64': edge_attr_64, 'edge_type_10': edge_type_10, 'edge_type_8': edge_type_8, 'L0_gnn_W_l1': _L0_gnn_in['W_l1'], 'L0_gnn_b1': _L0_gnn_in['b1'], 'L0_gnn_W_r1': _L0_gnn_in['W_r1'], 'L0_gnn_W_l2': _L0_gnn_in['W_l2'], 'L0_gnn_b2': _L0_gnn_in['b2'], 'L0_gnn_W_r2': _L0_gnn_in['W_r2'], 'L2_gnn_edge_matrix': _L2_gnn_in['edge_matrix'], 'L2_gnn_w_ih': _L2_gnn_in['w_ih'], 'L2_gnn_w_hh': _L2_gnn_in['w_hh'], 'L2_gnn_b_ih': _L2_gnn_in['b_ih'], 'L2_gnn_b_hh': _L2_gnn_in['b_hh'], 'L3_gnn_relation_weight': _L3_gnn_in['relation_weight'], 'L3_gnn_res_fc_w': _L3_gnn_in['res_fc_w'], 'L3_gnn_res_fc2_w': _L3_gnn_in['res_fc2_w']}

def reference(x, src, dst, edge_attr_64, edge_type_10, edge_type_8, L0_gnn_W_l1, L0_gnn_b1, L0_gnn_W_r1, L0_gnn_W_l2, L0_gnn_b2, L0_gnn_W_r2, L2_gnn_edge_matrix, L2_gnn_w_ih, L2_gnn_w_hh, L2_gnn_b_ih, L2_gnn_b_hh, L3_gnn_relation_weight, L3_gnn_res_fc_w, L3_gnn_res_fc2_w):
    import jax
    import jax.numpy as jnp

    def _L0_gnn_ref(x, edge_index, W_l1, b1, W_r1, W_l2, b2, W_r2):
        import jax, jax.numpy as jnp
        import numpy as np
        N_NODES = 12500
        N_EDGES = 200000
        IN_FEAT = 64
        HIDDEN = 64

        def _sage_conv(h, src, dst, W_l, b, W_r):
            n = h.shape[0]
            msg = h[src]
            agg = jax.ops.segment_sum(msg, dst, num_segments=n)
            cnt = jax.ops.segment_sum(jnp.ones((src.shape[0],), h.dtype), dst, num_segments=n)
            mean = agg / jnp.maximum(cnt, 1.0)[:, None]
            return mean @ W_l.T + b + h @ W_r.T
        src, dst = (edge_index[0], edge_index[1])
        h = jax.nn.relu(_sage_conv(x, src, dst, W_l1, b1, W_r1))
        return jax.nn.relu(_sage_conv(h, src, dst, W_l2, b2, W_r2))

    def _L1_gnn_ref(emb, edge_index):
        import jax, jax.numpy as jnp
        import numpy as np
        NUM_NODES = 12500
        EMBED_DIM = 64
        NUM_LAYERS = 3
        NUM_EDGES = 400000

        def _lightgcn_embedding(emb, edge_index):
            n = emb.shape[0]
            src, dst = (edge_index[0], edge_index[1])
            deg = jax.ops.segment_sum(jnp.ones(src.shape[0], dtype=emb.dtype), dst, num_segments=n)
            deg_inv_sqrt = jnp.where(deg > 0, jax.lax.rsqrt(jnp.maximum(deg, 1.0)), 0.0)
            w = deg_inv_sqrt[src] * deg_inv_sqrt[dst]
            x = emb
            out = emb
            for _ in range(NUM_LAYERS):
                x = jax.ops.segment_sum(w[:, None] * x[src], dst, num_segments=n)
                out = out + x
            return out / (NUM_LAYERS + 1)
        return _lightgcn_embedding(emb, edge_index)

    def _L2_gnn_ref(h, edge_matrix, w_ih, w_hh, b_ih, b_hh, edge_src, edge_dst, edge_type):
        import jax, jax.numpy as jnp
        import numpy as np
        N_NODES = 12500
        N_EDGES = 160000
        HID = 64
        MSG = 64
        N_ETYPE = 8

        def _ggnn_forward(h, edge_matrix, w_ih, w_hh, b_ih, b_hh, edge_src, edge_dst, edge_type):
            N, H = h.shape
            T = edge_matrix.shape[0]
            M = edge_matrix.shape[1] // H
            A = edge_matrix.reshape(T, M, H)
            Ht = jnp.einsum('tmh,nh->tnm', A, h)
            msg = Ht[edge_type, edge_src]
            m_agg = jax.ops.segment_sum(msg, edge_dst, num_segments=N)
            gi = m_agg @ w_ih.T + b_ih
            gh = h @ w_hh.T + b_hh
            i_r, i_z, i_n = (gi[:, :H], gi[:, H:2 * H], gi[:, 2 * H:])
            h_r, h_z, h_n = (gh[:, :H], gh[:, H:2 * H], gh[:, 2 * H:])
            r = jax.nn.sigmoid(i_r + h_r)
            z = jax.nn.sigmoid(i_z + h_z)
            n = jnp.tanh(i_n + r * h_n)
            return (1.0 - z) * n + z * h
        return _ggnn_forward(h, edge_matrix, w_ih, w_hh, b_ih, b_hh, edge_src, edge_dst, edge_type)

    def _L3_gnn_ref(nfeat, efeat, relation_weight, res_fc_w, res_fc2_w, src, dst, etype):
        import jax, jax.numpy as jnp
        import numpy as np
        NEG_SLOPE = 0.01
        N_NODES = 12500
        N_EDGES = 156250
        N_REL = 10
        D = 64
        n = nfeat.shape[0]
        proj = jnp.einsum('ni,rio->nro', nfeat, relation_weight)
        t_r = proj[src, etype]
        h_r = proj[dst, etype]
        att = jnp.sum(t_r * jnp.tanh(h_r + efeat), axis=-1)
        seg_max = jax.ops.segment_max(att, dst, num_segments=n)
        ex = jnp.exp(att - seg_max[dst])
        seg_sum = jax.ops.segment_sum(ex, dst, num_segments=n)
        a = ex / seg_sum[dst]
        h_nb = jax.ops.segment_sum(nfeat[src] * a[:, None], dst, num_segments=n)
        out = jax.nn.leaky_relu((nfeat + h_nb) @ res_fc_w.T, NEG_SLOPE) + jax.nn.leaky_relu(nfeat * h_nb @ res_fc2_w.T, NEG_SLOPE)
        return out
    edge_index = jnp.stack([src, dst])
    h = jnp.maximum(_layernorm(x, axis=-1), 0.0)
    x = x + _L0_gnn_ref(h, edge_index, L0_gnn_W_l1, L0_gnn_b1, L0_gnn_W_r1, L0_gnn_W_l2, L0_gnn_b2, L0_gnn_W_r2)
    h = jnp.maximum(_layernorm(x, axis=-1), 0.0)
    x = x + _L1_gnn_ref(h, edge_index)
    h = jnp.maximum(_layernorm(x, axis=-1), 0.0)
    x = x + _L2_gnn_ref(h, L2_gnn_edge_matrix, L2_gnn_w_ih, L2_gnn_w_hh, L2_gnn_b_ih, L2_gnn_b_hh, src, dst, edge_type_8)
    h = jnp.maximum(_layernorm(x, axis=-1), 0.0)
    x = x + _L3_gnn_ref(h, edge_attr_64, L3_gnn_relation_weight, L3_gnn_res_fc_w, L3_gnn_res_fc2_w, src, dst, edge_type_10)
    return x

_drawn_inputs = setup_inputs


def setup_inputs(seed=0):
    import zlib

    import numpy as np

    out = dict(_drawn_inputs(seed))
    spreads = {'L0_gnn_b1': (0.0, 0.1), 'L0_gnn_b2': (0.0, 0.1)}
    factors = {'L2_gnn_b_hh': 3.214}
    for name, (base, spread) in spreads.items():
        noise = np.random.default_rng([zlib.crc32(name.encode()), seed]).standard_normal(out[name].shape)
        drawn = base * np.exp(spread * noise) if base else spread * noise
        out[name] = jnp.asarray(drawn.astype(out[name].dtype))
    for name, factor in factors.items():
        out[name] = (out[name] * factor).astype(out[name].dtype)
    return out
```

```python
import concourse.bass as bass
import concourse.mybir as mybir
from contextlib import ExitStack

P = 128
D = 64
TILES = 8
GROUP = 7
R_GRU = 8
R_ATT = 10
ROW = 2 * D + 1
EPS = 1e-5
SLOPE = 0.01
FAR = -3.0e38
LOW = -1.0e30


def build(nc, x, src, dst, dst_rows, type8, type10, edge_attr, w_sage1, w_sage2, b_sage1, b_sage2,
          w_types8, w_gru, b_ih, b_hh, w_types10, w_res, identity, out):
    fp32, i32 = mybir.dt.float32, mybir.dt.int32
    ALU, ACT, AX = mybir.AluOpType, mybir.ActivationFunctionType, mybir.AxisListType
    nodes = x.shape[0]
    W = nodes // P
    NG = W // GROUP
    chunks = dst_rows.shape[0] * 2
    PAIRS = chunks // 2
    EDGES = TILES * P

    table = nc.dram_tensor("node_table", [nodes, D], fp32).ap()
    table8 = nc.dram_tensor("type_table8", [nodes * R_GRU, D], fp32).ap()
    table10 = nc.dram_tensor("type_table10", [nodes * R_ATT, 2 * D], fp32).ap()
    bounds_dram = nc.dram_tensor("bounds_dram", [PAIRS, 4], i32).ap()

    ctx = ExitStack()
    with ctx:
        def sb(name, shape, dt=fp32):
            return ctx.enter_context(nc.sbuf_tensor(name, shape, dt))

        def pb(name, shape):
            return ctx.enter_context(nc.psum_tensor(name, shape, fp32))

        def sem(name):
            return ctx.enter_context(nc.semaphore(name))

        x_sb = sb("x_sb", [P, W, D])
        h_sb = sb("h_sb", [P, W, D])
        y_sb = sb("y_sb", [P, W, D])
        acc = sb("acc", [P, W, D + 1])
        src_idx = sb("src_idx", [P, (chunks + 2) * TILES], i32)
        dst_idx = sb("dst_idx", [P, (chunks + 2) * TILES], i32)
        type_idx = y_sb[:, :, :].rearrange("p w d -> p (w d)")[:, 0:(chunks + 2) * TILES].bitcast(i32)
        dst_f = sb("dst_f", [P, chunks * TILES])
        staged_src = sb("staged_src", [P, 2, TILES], i32)
        staged_dst = sb("staged_dst", [P, 2, TILES], i32)
        rows = sb("rows", [P, 2, TILES, ROW])
        dst_proj = sb("dst_proj", [P, 2, TILES, D])
        attr = sb("attr", [P, 2, TILES, D])
        dst_wide = sb("dst_wide", [P, 2, EDGES], i32)
        onehot = sb("onehot", [P, TILES, P])
        scores = sb("scores", [P, EDGES])
        weights = sb("weights", [P, EDGES])
        att = sb("att", [P, TILES])
        node_max = sb("node_max", [P, W])
        step_max = sb("step_max", [P, 1])
        new_max = sb("new_max", [P, 1])
        neg_max = sb("neg_max", [P, 1])
        rescale = sb("rescale", [P, 1])
        stat = sb("stat", [P, W])
        stat2 = sb("stat2", [P, W])
        inv_sqrt_deg = sb("inv_sqrt_deg", [P, W])
        cat = sb("cat", [P, GROUP, 2 * D])
        cat_t = sb("cat_t", [P, GROUP * P])
        gates = sb("gates", [P, GROUP, 4 * D])
        hid = sb("hid", [P, GROUP, D])
        hid2 = sb("hid2", [P, GROUP, D])
        table_rows = sb("table_rows", [P, 2, R_ATT, 2 * D])
        chunk_dst = table_rows[0:PAIRS, :, :, :].rearrange("p a b c -> p (a b c)")[:, 0:2 * EDGES].bitcast(i32)\
            .rearrange("p (c e) -> p c e", c=2)
        bounds = sb("bounds", [PAIRS, 4], i32)
        bounds_row = sb("bounds_row", [1, PAIRS * 4], i32)
        lanes_i = sb("lanes_i", [P, P], i32)
        lanes = sb("lanes", [P, P])
        ids_i = sb("ids_i", [P, 2, W], i32)
        window_start = sb("window_start", [P, W])
        node_id = sb("node_id", [P, W])
        ident = sb("ident", [P, P])
        w1_sb = sb("w1_sb", [2 * D, D])
        w2_sb = sb("w2_sb", [2 * D, D])
        w8_sb = sb("w8_sb", [D, R_GRU * D])
        w10_sb = sb("w10_sb", [D, R_ATT * D])
        wg_sb = sb("wg_sb", [2 * D, 4 * D])
        wr_sb = sb("wr_sb", [2 * D, 2 * D])
        b1_sb = sb("b1_sb", [P, D])
        b2_sb = sb("b2_sb", [P, D])
        bg_sb = sb("bg_sb", [P, 4 * D])
        bh_sb = sb("bh_sb", [P, 3 * D])

        turned_ps = pb("turned_ps", [P, 1024])
        prod_ps = pb("prod_ps", [P, 2048])
        sums_ps = pb("sums_ps", [P, D + 1])

        const_loaded = sem("const_loaded")
        iota_done = sem("iota_done")
        setup_done = sem("setup_done")
        bounds_found = sem("bounds_found")
        bounds_saved = sem("bounds_saved")
        bounds_loaded = sem("bounds_loaded")
        dst_loaded = sem("dst_loaded")
        types_loaded = sem("types_loaded")
        types_wanted = sem("types_wanted")
        idx_ready = sem("idx_ready")
        var_ready = sem("var_ready")
        std_ready = sem("std_ready")
        rows_wanted = sem("rows_wanted")
        out_written = sem("out_written")
        dve_done = sem("dve_done")
        apart = {e: sem(f"apart_{e}") for e in ("sync", "pool", "act", "dve", "pe")}

        def stand_alone(engine, name):
            engine.sem_inc(apart[name], 1)

        class Chain:

            def __init__(self, eng):
                self.eng, self.base, self.n = eng, 0, 0

            def link(self, ins):
                self.n += 1
                ins.then_inc(dve_done, 1)
                self.eng.wait_ge(dve_done, self.base + self.n)

        def stage(name, names):
            return {n: sem(f"{name}_{n}") for n in names}

        PASS = ["table_ready", "table_written", "staged", "gathered0", "gathered1", "ring_free0", "ring_free1",
                "onehot_ready", "sums_ready", "acc_added"]
        NODE = ["cat_ready", "turned", "copied", "multiplied", "taken"]
        TABLE = ["picked", "turned", "copied"] + [f"{a}{k}" for a in ("projected", "rows_ready", "rows_written")
                                                  for k in range(2)]
        passes = [stage(f"pass{n}", PASS) for n in range(5)] + [stage("pass5", PASS[2:])]
        sages = [stage(f"sage{n}", NODE) for n in range(2)]
        gru = stage("gru", NODE + ["gates_ready", "squashed", "mixed", "new_ready", "cand_ready"])
        final = stage("final", NODE)
        tab8 = stage("tab8", TABLE)
        tab10 = stage("tab10", TABLE)
        attn = stage("attn", PASS[2:] + ["attr_loaded0", "attr_loaded1", "dst_loaded0", "dst_loaded1", "summed",
                                         "squashed", "scaled", "score_ready", "spread", "far_ready", "masked",
                                         "max_ready", "neg_ready", "rescale_ready", "exp_ready", "max_kept",
                                         "turned", "copied"])

        block = ctx.enter_context(nc.Block())

        by_window = table.rearrange("(w p) d -> p w d", p=P)

        def load_bounds(eng, regs, i):
            eng.load(regs, bounds_row[0:1, bass.ds(i * 4, 4)])

        def windows(eng, regs, par):
            return eng.Fori(eng.snap(regs[2 * par], min_val=0, max_val=W - 1),
                            eng.snap(regs[2 * par + 1], min_val=1, max_val=W))

        @block.sync
        def _(sp):
            sp.dma_start(chunk_dst, dst_rows.rearrange("p c e -> p c e")).then_inc(dst_loaded, 16)
            sp.dma_start(x_sb[:, :, :], x.rearrange("(w p) d -> p w d", p=P)).then_inc(const_loaded, 16)
            sp.dma_start(dst_idx[:, :], dst).then_inc(const_loaded, 16)
            sp.dma_start(src_idx[:, :], src).then_inc(const_loaded, 16)
            for to, of in ((ident, identity), (w1_sb, w_sage1), (w2_sb, w_sage2), (w8_sb, w_types8),
                           (w10_sb, w_types10), (wg_sb, w_gru), (wr_sb, w_res)):
                sp.dma_start(to[:, :], of).then_inc(const_loaded, 16)
            for to, of in ((b1_sb[:, :], b_sage1), (b2_sb[:, :], b_sage2), (bg_sb[:, 0:3 * D], b_ih),
                           (bh_sb[:, :], b_hh), (bg_sb[:, 3 * D:4 * D], b_hh[:, 2 * D:3 * D])):
                sp.dma_start(to, of.to_broadcast([P, of.shape[1]])).then_inc(const_loaded, 16)
            sp.wait_ge(bounds_found, 1)
            sp.dma_start(bounds_dram, bounds[:, :]).then_inc(bounds_saved, 16)
            sp.wait_ge(bounds_saved, 16)
            sp.dma_start(bounds_row[:, :], bounds_dram.rearrange("(o i) b -> o (i b)", o=1))\
              .then_inc(bounds_loaded, 16)

            for n in range(5):
                s = passes[n]
                sp.wait_ge(s["table_ready"], 1)
                sp.dma_start(by_window, (h_sb if n < 2 else y_sb)[:, :, :]).then_inc(s["table_written"], 16)
                if n < 2:
                    sp.wait_ge(s["table_written"], 16)

            def write_table(s, to, R, width):
                rows_of = to.rearrange("(w p r) d -> w p (r d)", p=P, r=R)
                with sp.Fori(0, W // 2) as j:
                    for k in range(2):
                        sp.wait_ge(s[f"rows_ready{k}"], (3 if width > D else 2) * (j + 1))
                        sp.dma_start(rows_of[bass.ds(2 * j + k, 1), :, :].rearrange("o p f -> (o p) f"),
                                     table_rows[:, k, :, :].rearrange("p r d -> p (r d)")[:, 0:R * width])\
                          .then_inc(s[f"rows_written{k}"], 16)

            sp.wait_ge(types_wanted, 1)
            sp.dma_start(type_idx, type8).then_inc(types_loaded, 16)
            write_table(tab8, table8, R_GRU, D)
            sp.wait_ge(types_wanted, 2)
            sp.dma_start(type_idx, type10).then_inc(types_loaded, 16)
            sp.dma_start(src_idx[:, :], src).then_inc(types_loaded, 16)
            write_table(tab10, table10, R_ATT, 2 * D)

            def attention_inputs(i, par, first):
                if not first:
                    sp.wait_ge(attn[f"ring_free{par}"], i)
                sp.dma_start(attr[:, par, :, :],
                             edge_attr[bass.ds(2 * i + par, 1), :, :, :].rearrange("o p t d -> (o p) t d"))\
                  .then_inc(attn[f"attr_loaded{par}"], 16)
                sp.dma_start(dst_wide[:, par, :],
                             dst_rows[bass.ds(i, 1), par, :].to_broadcast([P, EDGES]))\
                  .then_inc(attn[f"dst_loaded{par}"], 16)

            for par in range(2):
                attention_inputs(0, par, True)
            with sp.Fori(1, PAIRS) as i:
                for par in range(2):
                    attention_inputs(i, par, False)

            sp.wait_ge(rows_wanted, 1)
            sp.dma_start(out.rearrange("(w p) d -> p w d", p=P), x_sb[:, :, :]).then_inc(out_written, 16)
            sp.wait_ge(out_written, 16)

        @block.gpsimd
        def _(pool):
            pool.iota(lanes_i[:, :], pattern=[[1, P]], base=0, channel_multiplier=0).then_inc(iota_done, 1)
            pool.iota(ids_i[:, 0, :], pattern=[[P, W]], base=0, channel_multiplier=0).then_inc(iota_done, 1)
            pool.iota(ids_i[:, 1, :], pattern=[[P, W]], base=0, channel_multiplier=1).then_inc(iota_done, 1)
            pool.memset(rows[:, :, :, 2 * D:ROW], 1.0).then_inc(iota_done, 1)

            def gather(par, t, from_, idx, to, s):
                pool.indirect_dma_start(out=to, out_offset=None, in_=from_,
                                        in_offset=bass.IndirectOffsetOnAxis(ap=idx[:, par, t:t + 1], axis=0))\
                    .then_inc(s[f"gathered{par}"], 16)

            def gather_pass(s, chunk):
                for par in range(2):
                    pool.wait_ge(s["staged"], par + 1)
                    chunk(par)
                with pool.Fori(1, PAIRS) as i:
                    for par in range(2):
                        pool.wait_ge(s["staged"], 2 * i + par + 1)
                        pool.wait_ge(s[f"ring_free{par}"], i)
                        stand_alone(pool, "pool")
                        chunk(par)

            def plain_pass(s, from_):
                def chunk(par):
                    for t in range(TILES):
                        gather(par, t, from_, staged_src, rows[:, par, t, D:2 * D], s)
                gather_pass(s, chunk)

            for n in range(5):
                pool.wait_ge(passes[n]["table_written"], 16)
                plain_pass(passes[n], table)
            for k in range(2):
                pool.wait_ge(tab8[f"rows_written{k}"], 16 * (W // 2))
            plain_pass(passes[5], table8)

            def copy_nodes(j, k, first):
                if first:
                    pool.wait_ge(tab10["picked"], 1)
                else:
                    pool.wait_ge(tab10["picked"], j + 1)
                    pool.wait_ge(tab10[f"rows_written{k}"], 16 * j)
                    stand_alone(pool, "pool")
                pool.tensor_copy(table_rows[:, k, :, D:2 * D],
                                 h_sb[:, bass.ds(2 * j + k, 1), :].to_broadcast([P, R_ATT, D]))\
                    .then_inc(tab10[f"rows_ready{k}"], 1)

            for k in range(2):
                copy_nodes(0, k, True)
            with pool.Fori(1, W // 2) as j:
                for k in range(2):
                    copy_nodes(j, k, False)

            for k in range(2):
                pool.wait_ge(tab10[f"rows_written{k}"], 16 * (W // 2))
            halves = table10.rearrange("n (b d) -> (n b) d", b=2)

            def attention_chunk(par):
                for t in range(TILES):
                    gather(par, t, table10, staged_src, rows[:, par, t, 0:2 * D], attn)
                    gather(par, t, halves, staged_dst, dst_proj[:, par, t, :], attn)
            gather_pass(attn, attention_chunk)

        @block.scalar
        def _(act):
            def stage_indices(s, m, par, pairs):
                for to, of in pairs[:-1]:
                    act.activation(to[:, par, :], of[:, bass.ds(m * TILES, TILES)], ACT.Copy)
                to, of = pairs[-1]
                act.activation(to[:, par, :], of[:, bass.ds(m * TILES, TILES)], ACT.Copy).then_inc(s["staged"], 1)

            def plain_pass(s):
                pairs = [(staged_src, src_idx)]
                for par in range(2):
                    stage_indices(s, par, par, pairs)
                with act.Fori(0, PAIRS) as i:
                    for par in range(2):
                        act.wait_ge(s[f"gathered{par}"], 16 * TILES * (i + 1))
                        stand_alone(act, "act")
                        stage_indices(s, 2 * i + par + 2, par, pairs)
                act.wait_ge(s["staged"], 2 * PAIRS + 2)

            def norm(n):
                act.wait_ge(var_ready, n)
                act.activation(stat2[:, :], stat[:, :], ACT.Sqrt).then_inc(std_ready, 1)

            def each_group(one):
                one(0, True)
                with act.Fori(1, NG) as g:
                    one(g, False)

            def copy_turned(s):
                def one(g, first):
                    act.wait_ge(s["turned"], g + 1)
                    act.activation(cat_t[:, :], turned_ps[:, 0:GROUP * P], ACT.Copy).then_inc(s["copied"], 1)
                return one

            def make_table(s, R, width):
                half = R * D // 2

                def one(j, first):
                    if not first:
                        act.wait_ge(s["turned"], j)
                        stand_alone(act, "act")
                    act.activation(cat[:, 0:2, 0:D], h_sb[:, bass.ds(2 * j, 2), :], ACT.Copy).then_inc(s["picked"], 1)
                    act.wait_ge(s["turned"], j + 1)
                    act.activation(cat_t[0:D, 0:2 * P], turned_ps[0:D, 0:2 * P], ACT.Copy).then_inc(s["copied"], 1)
                    for k in range(2):
                        act.wait_ge(s[f"projected{k}"], j + 1)
                        if not first:
                            act.wait_ge(s[f"rows_written{k}"], 16 * j)
                            stand_alone(act, "act")
                        act.activation(table_rows[:, k, :, :].rearrange("p r d -> p (r d)")[:, 0:R * width]
                                       .rearrange("p (r d) -> p r d", r=R)[:, R // 2:R, 0:D],
                                       prod_ps[:, (2 * k + 1) * 512:(2 * k + 1) * 512 + half]
                                       .rearrange("p (r d) -> p r d", d=D), ACT.Copy)\
                           .then_inc(s[f"rows_ready{k}"], 1)
                one(0, True)
                with act.Fori(1, W // 2) as j:
                    one(j, False)

            act.wait_ge(const_loaded, 16 * 15)
            norm(1)
            plain_pass(passes[0])
            each_group(copy_turned(sages[0]))
            plain_pass(passes[1])
            each_group(copy_turned(sages[1]))
            norm(2)
            norm(3)
            for n in (2, 3, 4):
                plain_pass(passes[n])
            norm(4)
            act.wait_ge(idx_ready, 1)
            make_table(tab8, R_GRU, D)
            plain_pass(passes[5])

            def gru_group(g, first):
                copy_turned(gru)(g, first)
                act.wait_ge(gru["gates_ready"], g + 1)
                act.activation(gates[:, :, 0:2 * D], gates[:, :, 0:2 * D], ACT.Tanh, scale=0.5)\
                   .then_inc(gru["squashed"], 1)
                act.wait_ge(gru["cand_ready"], g + 1)
                act.activation(hid[:, :, :], hid[:, :, :], ACT.Tanh).then_inc(gru["new_ready"], 1)
            each_group(gru_group)
            norm(5)
            act.wait_ge(idx_ready, 2)
            make_table(tab10, R_ATT, 2 * D)

            pairs = [(staged_src, src_idx), (staged_dst, dst_idx)]
            for par in range(2):
                stage_indices(attn, par, par, pairs)
            lo_hi = [act.alloc_register(f"act_bound{k}") for k in range(4)]
            steps = act.alloc_register("act_steps")
            act.reg_mov(steps, 0)
            with act.Fori(0, PAIRS) as i:
                load_bounds(act, lo_hi, i)
                for par in range(2):
                    m = 2 * i + par
                    act.wait_ge(attn[f"gathered{par}"], 32 * TILES * (i + 1))
                    stand_alone(act, "act")
                    stage_indices(attn, m + 2, par, pairs)
                    act.wait_ge(attn["summed"], m + 1)
                    act.activation(dst_proj[:, par, :, :], dst_proj[:, par, :, :], ACT.Tanh)\
                       .then_inc(attn["squashed"], 1)
                    with windows(act, lo_hi, par) as n:
                        s = act.snap(steps)
                        act.wait_ge(attn["neg_ready"], s + 1)
                        stand_alone(act, "act")
                        act.activation(rescale[:, :], node_max[:, bass.ds(n, 1)], ACT.Exp, bias=neg_max[:, 0:1])\
                           .then_inc(attn["rescale_ready"], 1)
                        act.activation(scores[:, :], scores[:, :], ACT.Exp, bias=neg_max[:, 0:1])\
                           .then_inc(attn["exp_ready"], 1)
                        act.wait_ge(attn["turned"], s + 1)
                        act.activation(weights[:, :], turned_ps[:, :], ACT.Copy).then_inc(attn["copied"], 1)
                        act.reg_add(steps, steps, 1)
            each_group(copy_turned(final))

        @block.tensor
        def _(pe):
            pe.wait_ge(const_loaded, 16 * 15)
            pe.wait_ge(bounds_loaded, 16)
            lo_hi = [pe.alloc_register(f"pe_bound{k}") for k in range(4)]
            steps = pe.alloc_register("pe_steps")

            def sum_edges(s, par, lhs):
                for t in range(TILES):
                    last = pe.matmul(sums_ps[:, :], lhs(t), rows[:, par, t, D:ROW],
                                     start=(t == 0), stop=(t == TILES - 1))
                last.then_inc(s["sums_ready"], 1)

            def plain_pass(s):
                pe.reg_mov(steps, 0)
                with pe.Fori(0, PAIRS) as i:
                    load_bounds(pe, lo_hi, i)
                    for par in range(2):
                        pe.wait_ge(s[f"gathered{par}"], 16 * TILES * (i + 1))
                        stand_alone(pe, "pe")
                        with windows(pe, lo_hi, par) as _n:
                            st = pe.snap(steps)
                            pe.wait_ge(s["onehot_ready"], st + 1)
                            sum_edges(s, par, lambda t: onehot[:, t, :])
                            pe.reg_add(steps, steps, 1)
                        pe.drain().then_inc(s[f"ring_free{par}"], 1)

            def each_group(one):
                one(0, True)
                with pe.Fori(1, NG) as g:
                    one(g, False)

            def node_stage(s, w, cols, at):
                def one(g, first):
                    pe.wait_ge(s["cat_ready"], g + 1)
                    for k in range(GROUP):
                        last = pe.transpose(turned_ps[:, k * P:(k + 1) * P], cat[:, k, :], ident[:, :])
                    last.then_inc(s["turned"], 1)
                    pe.wait_ge(s["copied"], g + 1)
                    for k in range(GROUP):
                        last = pe.matmul(prod_ps[:, at(k):at(k) + cols], cat_t[:, k * P:(k + 1) * P], w[:, :],
                                         start=True, stop=True)
                    last.then_inc(s["multiplied"], 1)
                each_group(one)

            def make_table(s, w, R):
                half = R * D // 2

                def one(j, first):
                    pe.wait_ge(s["picked"], j + 1)
                    stand_alone(pe, "pe")
                    for k in range(2):
                        last = pe.transpose(turned_ps[0:D, k * P:(k + 1) * P], cat[:, k, 0:D], ident[:, :])
                    last.then_inc(s["turned"], 1)
                    pe.wait_ge(s["copied"], j + 1)
                    for k in range(2):
                        if not first:
                            pe.wait_ge(s[f"rows_ready{k}"], (3 if R == R_ATT else 2) * j)
                        for b in range(2):
                            c = (2 * k + b) * 512
                            last = pe.matmul(prod_ps[:, c:c + half], cat_t[0:D, k * P:(k + 1) * P],
                                             w[:, b * half:(b + 1) * half], start=True, stop=True)
                        last.then_inc(s[f"projected{k}"], 1)
                one(0, True)
                with pe.Fori(1, W // 2) as j:
                    one(j, False)

            def side_by_side(cols):
                per_bank = 512 // cols
                return lambda k: (k // per_bank) * 512 + (k % per_bank) * cols

            plain_pass(passes[0])
            node_stage(sages[0], w1_sb, D, side_by_side(D))
            plain_pass(passes[1])
            node_stage(sages[1], w2_sb, D, side_by_side(D))
            for n in (2, 3, 4):
                plain_pass(passes[n])
            make_table(tab8, w8_sb, R_GRU)
            plain_pass(passes[5])
            node_stage(gru, wg_sb, 4 * D, side_by_side(4 * D))
            make_table(tab10, w10_sb, R_ATT)

            pe.reg_mov(steps, 0)
            with pe.Fori(0, PAIRS) as i:
                load_bounds(pe, lo_hi, i)
                for par in range(2):
                    pe.wait_ge(attn["score_ready"], 2 * i + par + 1)
                    for t in range(TILES):
                        last = pe.matmul(prod_ps[:, t * P:(t + 1) * P], att[:, t:t + 1].to_broadcast([P, P]),
                                         ident[:, :], start=True, stop=True)
                    last.then_inc(attn["spread"], 1)
                    with windows(pe, lo_hi, par) as _n:
                        st = pe.snap(steps)
                        pe.wait_ge(attn["exp_ready"], st + 1)
                        for t in range(TILES):
                            last = pe.transpose(turned_ps[:, t * P:(t + 1) * P], scores[:, t * P:(t + 1) * P],
                                                ident[:, :])
                        last.then_inc(attn["turned"], 1)
                        pe.wait_ge(attn["copied"], st + 1)
                        sum_edges(attn, par, lambda t: weights[:, t * P:(t + 1) * P])
                        pe.reg_add(steps, steps, 1)
                    pe.drain().then_inc(attn[f"ring_free{par}"], 1)
            node_stage(final, wr_sb, 2 * D, side_by_side(2 * D))

        @block.vector
        def _(dve):
            chain = Chain(dve)
            link = chain.link
            lo_hi = [dve.alloc_register(f"dve_bound{k}") for k in range(4)]
            steps = dve.alloc_register("dve_steps")

            def per_node(v):
                return v.unsqueeze(2).to_broadcast([P, v.shape[1], D])

            dve.wait_ge(dst_loaded, 16)
            lohi = bounds[:, :].rearrange("p (c b) -> p c b", b=2)
            link(dve.tensor_reduce(lohi[:, :, 0], chunk_dst, AX.X, ALU.min))
            link(dve.tensor_reduce(lohi[:, :, 1], chunk_dst, AX.X, ALU.max))
            link(dve.tensor_scalar(bounds[:, :], bounds[:, :], 7, None, ALU.arith_shift_right))
            dve.tensor_scalar(lohi[:, :, 1], lohi[:, :, 1], 1.0, None, ALU.add).then_inc(bounds_found, 1)
            dve.wait_ge(iota_done, 4)
            link(dve.tensor_copy(lanes[:, :], lanes_i[:, :]))
            link(dve.tensor_copy(window_start[:, :], ids_i[:, 0, :]))
            link(dve.tensor_copy(node_id[:, :], ids_i[:, 1, :]))
            dve.wait_ge(const_loaded, 16 * 15)
            link(dve.tensor_copy(dst_f[:, :], dst_idx[:, 0:chunks * TILES]))
            link(dve.tensor_tensor(bg_sb[:, 0:2 * D], bg_sb[:, 0:2 * D], bh_sb[:, 0:2 * D], ALU.add))
            dve.wait_ge(bounds_loaded, 16)

            def layer_norm(n, last=None):
                link(dve.tensor_reduce(stat[:, :], x_sb[:, :, :], AX.X, ALU.add))
                link(dve.tensor_scalar(stat[:, :], stat[:, :], 1.0 / D, None, ALU.mult))
                link(dve.tensor_tensor(y_sb[:, :, :], x_sb[:, :, :], per_node(stat[:, :]), ALU.subtract))
                link(dve.tensor_tensor(h_sb[:, :, :], y_sb[:, :, :], y_sb[:, :, :], ALU.mult))
                link(dve.tensor_reduce(stat[:, :], h_sb[:, :, :], AX.X, ALU.add))
                dve.tensor_scalar(stat[:, :], stat[:, :], 1.0 / D, EPS, ALU.mult, ALU.add).then_inc(var_ready, 1)
                dve.wait_ge(std_ready, n)
                link(dve.reciprocal(stat[:, :], stat2[:, :]))
                ins = dve.scalar_tensor_tensor(h_sb[:, :, :], y_sb[:, :, :], 0.0, per_node(stat[:, :]),
                                               ALU.max, ALU.mult)
                if last is None:
                    link(ins)
                else:
                    ins.then_inc(last, 1)
                    dve.wait_ge(last, 1)

            def plain_pass(s):
                dve.memset(acc[:, :, :], 0.0).then_inc(s["acc_added"], 1)
                dve.reg_mov(steps, 0)
                with dve.Fori(0, PAIRS) as i:
                    load_bounds(dve, lo_hi, i)
                    for par in range(2):
                        with windows(dve, lo_hi, par) as n:
                            st = dve.snap(steps)
                            dve.wait_ge(s["acc_added"], st + 1)
                            here = dst_f[:, bass.ds((2 * i + par) * TILES, TILES)].unsqueeze(2)\
                                .to_broadcast([P, TILES, P])
                            dve.scalar_tensor_tensor(onehot[:, :, :], here, window_start[:, bass.ds(n, 1)],
                                                     lanes[:, :].unsqueeze(1).to_broadcast([P, TILES, P]),
                                                     ALU.subtract, ALU.is_equal).then_inc(s["onehot_ready"], 1)
                            dve.wait_ge(s["sums_ready"], st + 1)
                            at = acc[:, bass.ds(n, 1), :].rearrange("p o d -> p (o d)")
                            dve.tensor_tensor(at, at, sums_ps[:, :], ALU.add).then_inc(s["acc_added"], 1)
                            dve.reg_add(steps, steps, 1)
                dve.wait_ge(s["acc_added"], dve.snap(steps) + 1)
                stand_alone(dve, "dve")

            def each_group(one, links=0):
                one(0, True)
                start = chain.n + chain.base if links else 0
                with dve.Fori(1, NG) as g:
                    if links:
                        chain.base, chain.n = (g - 1) * links + start, 0
                    one(g, False)
                if links:
                    assert chain.n == links
                    chain.base, chain.n = 0, start + (NG - 1) * links

            def group(buf, g):
                return buf[:, bass.ds(g * GROUP, GROUP), 0:D]

            def ready_cat(s, g, fill):
                fill(g)

            def mean_sage(s, bias, put):
                link(dve.tensor_scalar(stat[:, :], acc[:, :, D], 1.0, None, ALU.max))
                link(dve.reciprocal(stat2[:, :], stat[:, :]))
                link(dve.tensor_tensor(y_sb[:, :, :], acc[:, :, 0:D], per_node(stat2[:, :]), ALU.mult))

                def one(g, first):
                    link(dve.tensor_copy(cat[:, :, 0:D], group(y_sb, g)))
                    dve.tensor_copy(cat[:, :, D:2 * D], group(h_sb, g)).then_inc(s["cat_ready"], 1)
                    dve.wait_ge(s["multiplied"], g + 1)
                    link(dve.tensor_tensor(hid[:, :, :], prod_ps[:, 0:GROUP * D].rearrange("p (k d) -> p k d", d=D),
                                           bias[:, :].unsqueeze(1).to_broadcast([P, GROUP, D]), ALU.add))
                    link(put(g))
                each_group(one, 3)

            layer_norm(1, passes[0]["table_ready"])
            plain_pass(passes[0])
            mean_sage(sages[0], b1_sb,
                      lambda g: dve.tensor_scalar(group(h_sb, g), hid[:, :, :], 0.0, None, ALU.max))
            dve.sem_inc(passes[1]["table_ready"], 1)
            plain_pass(passes[1])
            mean_sage(sages[1], b2_sb,
                      lambda g: dve.scalar_tensor_tensor(group(x_sb, g), hid[:, :, :], 0.0, group(x_sb, g),
                                                         ALU.max, ALU.add))

            layer_norm(2)
            link(dve.tensor_scalar(inv_sqrt_deg[:, :], acc[:, :, D], 1.0, None, ALU.min))
            dve.tensor_scalar(stat[:, :], acc[:, :, D], 1.0, None, ALU.max).then_inc(var_ready, 1)
            dve.wait_ge(std_ready, 3)
            link(dve.reciprocal(stat[:, :], stat2[:, :]))
            link(dve.tensor_tensor(inv_sqrt_deg[:, :], inv_sqrt_deg[:, :], stat[:, :], ALU.mult))
            for n in (2, 3, 4):
                link(dve.scalar_tensor_tensor(x_sb[:, :, :], h_sb[:, :, :], 0.25, x_sb[:, :, :], ALU.mult, ALU.add))
                dve.tensor_tensor(y_sb[:, :, :], h_sb[:, :, :], per_node(inv_sqrt_deg[:, :]), ALU.mult)\
                   .then_inc(passes[n]["table_ready"], 1)
                plain_pass(passes[n])
                link(dve.tensor_tensor(h_sb[:, :, :], acc[:, :, 0:D], per_node(inv_sqrt_deg[:, :]), ALU.mult))
            link(dve.scalar_tensor_tensor(x_sb[:, :, :], h_sb[:, :, :], 0.25, x_sb[:, :, :], ALU.mult, ALU.add))

            def make_table(s, R, width):
                half = R * D // 2

                def one(j, first):
                    for k in range(2):
                        dve.wait_ge(s[f"projected{k}"], j + 1)
                        if not first:
                            dve.wait_ge(s[f"rows_written{k}"], 16 * j)
                            stand_alone(dve, "dve")
                        dve.tensor_copy(table_rows[:, k, :, :].rearrange("p r d -> p (r d)")[:, 0:R * width]
                                        .rearrange("p (r d) -> p r d", r=R)[:, 0:R // 2, 0:D],
                                        prod_ps[:, 2 * k * 512:2 * k * 512 + half]
                                        .rearrange("p (r d) -> p r d", d=D)).then_inc(s[f"rows_ready{k}"], 1)
                one(0, True)
                with dve.Fori(1, W // 2) as j:
                    one(j, False)

            layer_norm(4)
            dve.sem_inc(types_wanted, 1)
            dve.wait_ge(types_loaded, 16)
            link(dve.tensor_scalar(src_idx[:, :], src_idx[:, :], float(R_GRU), None, ALU.mult))
            dve.tensor_tensor(src_idx[:, :], src_idx[:, :], type_idx, ALU.add).then_inc(idx_ready, 1)
            make_table(tab8, R_GRU, D)
            plain_pass(passes[5])

            def gru_one(g, first):
                link(dve.tensor_copy(cat[:, :, 0:D], group(acc, g)))
                dve.tensor_copy(cat[:, :, D:2 * D], group(h_sb, g)).then_inc(gru["cat_ready"], 1)
                dve.wait_ge(gru["multiplied"], g + 1)
                dve.tensor_tensor(gates[:, :, :], prod_ps[:, 0:GROUP * 4 * D].rearrange("p (k c) -> p k c", c=4 * D),
                                  bg_sb[:, :].unsqueeze(1).to_broadcast([P, GROUP, 4 * D]), ALU.add)\
                   .then_inc(gru["gates_ready"], 1)
                dve.wait_ge(gru["squashed"], g + 1)
                link(dve.scalar_tensor_tensor(hid[:, :, :], gates[:, :, 0:D], 1.0, gates[:, :, 3 * D:4 * D],
                                              ALU.add, ALU.mult))
                dve.scalar_tensor_tensor(hid[:, :, :], hid[:, :, :], 0.5, gates[:, :, 2 * D:3 * D],
                                         ALU.mult, ALU.add).then_inc(gru["cand_ready"], 1)
                dve.wait_ge(gru["new_ready"], g + 1)
                link(dve.tensor_tensor(hid2[:, :, :], group(h_sb, g), hid[:, :, :], ALU.subtract))
                link(dve.scalar_tensor_tensor(hid2[:, :, :], gates[:, :, D:2 * D], 1.0, hid2[:, :, :],
                                              ALU.add, ALU.mult))
                link(dve.scalar_tensor_tensor(hid2[:, :, :], hid2[:, :, :], 0.5, hid[:, :, :], ALU.mult, ALU.add))
                link(dve.tensor_tensor(group(x_sb, g), group(x_sb, g), hid2[:, :, :], ALU.add))
            each_group(gru_one, 6)

            layer_norm(5)
            dve.sem_inc(types_wanted, 1)
            dve.wait_ge(types_loaded, 16 * 3)
            for idx in (src_idx, dst_idx):
                link(dve.tensor_scalar(idx[:, :], idx[:, :], float(R_ATT), None, ALU.mult))
                link(dve.tensor_tensor(idx[:, :], idx[:, :], type_idx, ALU.add))
            dve.tensor_scalar(dst_idx[:, :], dst_idx[:, :], 2.0, None, ALU.mult).then_inc(idx_ready, 1)
            make_table(tab10, R_ATT, 2 * D)

            link(dve.memset(node_max[:, :], LOW))
            dve.memset(acc[:, :, :], 0.0).then_inc(attn["acc_added"], 1)
            dve.reg_mov(steps, 0)
            with dve.Fori(0, PAIRS) as i:
                load_bounds(dve, lo_hi, i)
                for par in range(2):
                    m = 2 * i + par
                    proj = dst_proj[:, par, :, :]
                    dve.wait_ge(attn[f"gathered{par}"], 32 * TILES * (i + 1))
                    dve.wait_ge(attn[f"attr_loaded{par}"], 16 * (i + 1))
                    dve.tensor_tensor(proj, proj, attr[:, par, :, :], ALU.add).then_inc(attn["summed"], 1)
                    dve.wait_ge(attn["squashed"], m + 1)
                    dve.tensor_tensor(proj, proj, rows[:, par, :, 0:D], ALU.mult).then_inc(attn["scaled"], 1)
                    dve.wait_ge(attn["scaled"], m + 1)
                    dve.tensor_reduce(att[:, :], proj, AX.X, ALU.add).then_inc(attn["score_ready"], 1)
                    dve.wait_ge(attn["spread"], m + 1)
                    dve.wait_ge(attn[f"dst_loaded{par}"], 16 * (i + 1))
                    stand_alone(dve, "dve")
                    with windows(dve, lo_hi, par) as n:
                        st = dve.snap(steps)
                        dve.wait_ge(attn["acc_added"], st + 1)
                        dve.tensor_scalar(scores[:, :], dst_wide[:, par, :], node_id[:, bass.ds(n, 1)], FAR,
                                          ALU.not_equal, ALU.mult).then_inc(attn["far_ready"], 1)
                        dve.wait_ge(attn["far_ready"], st + 1)
                        stand_alone(dve, "dve")
                        dve.tensor_tensor_reduce(out=scores[:, :], in0=scores[:, :], in1=prod_ps[:, 0:EDGES],
                                                 scale=1.0, scalar=FAR, op0=ALU.add, op1=ALU.max,
                                                 accum_out=step_max[:, :]).then_inc(attn["masked"], 1)
                        dve.wait_ge(attn["masked"], st + 1)
                        dve.tensor_tensor(new_max[:, :], step_max[:, :], node_max[:, bass.ds(n, 1)], ALU.max)\
                           .then_inc(attn["max_ready"], 1)
                        dve.wait_ge(attn["max_ready"], st + 1)
                        dve.tensor_scalar(neg_max[:, :], new_max[:, :], -1.0, None, ALU.mult)\
                           .then_inc(attn["neg_ready"], 1)
                        dve.wait_ge(attn["rescale_ready"], st + 1)
                        stand_alone(dve, "dve")
                        dve.tensor_copy(node_max[:, bass.ds(n, 1)], new_max[:, :]).then_inc(attn["max_kept"], 1)
                        dve.wait_ge(attn["sums_ready"], st + 1)
                        at = acc[:, bass.ds(n, 1), :].rearrange("p o d -> p (o d)")
                        dve.scalar_tensor_tensor(at, at, rescale[:, 0:1], sums_ps[:, :], ALU.mult, ALU.add)\
                           .then_inc(attn["acc_added"], 1)
                        dve.reg_add(steps, steps, 1)
            dve.wait_ge(attn["acc_added"], dve.snap(steps) + 1)
            stand_alone(dve, "dve")
            link(dve.tensor_scalar(stat[:, :], acc[:, :, D], 1.0e-30, None, ALU.max))
            link(dve.reciprocal(stat2[:, :], stat[:, :]))
            link(dve.tensor_tensor(y_sb[:, :, :], acc[:, :, 0:D], per_node(stat2[:, :]), ALU.mult))

            def final_one(g, first):
                link(dve.tensor_tensor(cat[:, :, 0:D], group(y_sb, g), group(h_sb, g), ALU.add))
                dve.tensor_tensor(cat[:, :, D:2 * D], group(y_sb, g), group(h_sb, g), ALU.mult)\
                   .then_inc(final["cat_ready"], 1)
                dve.wait_ge(final["multiplied"], g + 1)
                both = gates[:, :, 0:2 * D]
                link(dve.tensor_copy(both, prod_ps[:, 0:GROUP * 2 * D].rearrange("p (k c) -> p k c", c=2 * D)))
                link(dve.scalar_tensor_tensor(both, both, SLOPE, both, ALU.mult, ALU.max))
                link(dve.tensor_tensor(group(x_sb, g), group(x_sb, g), gates[:, :, 0:D], ALU.add))
                link(dve.tensor_tensor(group(x_sb, g), group(x_sb, g), gates[:, :, D:2 * D], ALU.add))
            each_group(final_one, 5)
            dve.sem_inc(rows_wanted, 1)


def kernel(**inputs):
    import numpy as np
    import concourse.bacc as bacc
    from concourse.bass_utils import run_bass_kernel_spmd

    a = {k: np.asarray(v) for k, v in inputs.items()}
    n_nodes, n_edges = a["x"].shape[0], a["src"].shape[0]
    tile_group = P * GROUP * 2
    nodes = -(-n_nodes // tile_group) * tile_group
    edges = P * TILES
    pairs = -(-n_edges // (2 * edges))
    padded = pairs * 2 * edges
    tiles = padded // P

    def edge_list(v, fill):
        e = np.full([padded], fill, v.dtype)
        e[:n_edges] = v
        cols = np.zeros([P, tiles + 2 * TILES], v.dtype)
        cols[:, :tiles] = e.reshape(tiles, P).T
        return e, cols

    x = np.zeros([nodes, D], a["x"].dtype)
    x[:n_nodes] = a["x"]
    dst_flat, dst = edge_list(a["dst"], nodes - 1)
    attr = np.zeros([padded, D], a["edge_attr_64"].dtype)
    attr[:n_edges] = a["edge_attr_64"]
    T = lambda name: np.ascontiguousarray(a[name].T)
    w_ih, w_hh = T("L2_gnn_w_ih"), T("L2_gnn_w_hh")
    w_gru = np.zeros([2 * D, 4 * D], w_ih.dtype)
    w_gru[:D, :3 * D] = w_ih
    w_gru[D:, :2 * D] = w_hh[:, :2 * D]
    w_gru[D:, 3 * D:] = w_hh[:, 2 * D:]
    w_res = np.zeros([2 * D, 2 * D], w_ih.dtype)
    w_res[:D, :D] = T("L3_gnn_res_fc_w")
    w_res[D:, D:] = T("L3_gnn_res_fc2_w")
    arrays = {
        "x": x,
        "src": edge_list(a["src"], 0)[1],
        "dst": dst,
        "dst_rows": dst_flat.reshape(pairs, 2, edges),
        "type8": edge_list(a["edge_type_8"], 0)[1],
        "type10": edge_list(a["edge_type_10"], 0)[1],
        "edge_attr": np.ascontiguousarray(attr.reshape(2 * pairs, TILES, P, D).transpose(0, 2, 1, 3)),
        "w_sage1": np.concatenate([T("L0_gnn_W_l1"), T("L0_gnn_W_r1")]),
        "w_sage2": np.concatenate([T("L0_gnn_W_l2"), T("L0_gnn_W_r2")]),
        "b_sage1": a["L0_gnn_b1"][None, :],
        "b_sage2": a["L0_gnn_b2"][None, :],
        "w_types8": np.ascontiguousarray(a["L2_gnn_edge_matrix"].reshape(R_GRU, D, D).transpose(2, 0, 1)
                                         .reshape(D, R_GRU * D)),
        "w_gru": w_gru,
        "b_ih": a["L2_gnn_b_ih"][None, :],
        "b_hh": a["L2_gnn_b_hh"][None, :],
        "w_types10": np.ascontiguousarray(a["L3_gnn_relation_weight"].transpose(1, 0, 2).reshape(D, R_ATT * D)),
        "w_res": w_res,
        "identity": np.eye(P, dtype=np.float32),
    }
    nc = bacc.Bacc("TRN2", target_bir_lowering=False, num_devices=1)
    args = {n: nc.dram_tensor(f"in_{n}", v.shape, mybir.dt.from_np(v.dtype), kind="ExternalInput").ap()
            for n, v in arrays.items()}
    out = nc.dram_tensor("out", [nodes, D], mybir.dt.float32, kind="ExternalOutput").ap()
    build(nc, out=out, **args)
    r = run_bass_kernel_spmd(nc, [{f"in_{n}": v for n, v in arrays.items()}], core_ids=[0])
    return r.results[0]["out"][:n_nodes]
```

```python
import concourse.bass as bass
import concourse.mybir as mybir
from contextlib import ExitStack

P = 128
D = 64
TILES = 8
GROUP = 7
R_GRU = 8
R_ATT = 10
SLOTS = 4
HALF = TILES // 2
PARTS = 3
ROW = 2 * D + 1
EPS = 1e-5
SLOPE = 0.01
FAR = -3.0e38
LOW = -1.0e30


def build(nc, x, src, dst, dst_rows, type8, type10, edge_attr, w_sage1, w_sage2, b_sage1, b_sage2,
          w_types8, w_gru, b_ih, b_hh, w_types10, w_res, identity, out):
    fp32, i32, bf16 = mybir.dt.float32, mybir.dt.int32, mybir.dt.bfloat16
    ALU, ACT, AX = mybir.AluOpType, mybir.ActivationFunctionType, mybir.AxisListType
    nodes = x.shape[0]
    W = nodes // P
    NG = W // GROUP
    ROUNDS = dst_rows.shape[0]
    chunks = ROUNDS * SLOTS
    EDGES = TILES * P

    table = nc.dram_tensor("node_table", [nodes, PARTS * D], bf16).ap()
    table8 = nc.dram_tensor("type_table8", [nodes * R_GRU, PARTS * D], bf16).ap()
    table10 = nc.dram_tensor("type_table10", [nodes * R_ATT, 2 * D], fp32).ap()
    bounds_dram = nc.dram_tensor("bounds_dram", [ROUNDS, 2 * SLOTS], i32).ap()

    ctx = ExitStack()
    with ctx:
        def sb(name, shape, dt=fp32):
            return ctx.enter_context(nc.sbuf_tensor(name, shape, dt))

        def pb(name, shape):
            return ctx.enter_context(nc.psum_tensor(name, shape, fp32))

        def sem(name):
            return ctx.enter_context(nc.semaphore(name))

        x_sb = sb("x_sb", [P, W, D])
        h_sb = sb("h_sb", [P, W, D])
        y_sb = sb("y_sb", [P, W, D])
        acc = sb("acc", [P, W, D + 1])
        src_idx = sb("src_idx", [P, (chunks + SLOTS) * TILES], i32)
        dst_idx = sb("dst_idx", [P, (chunks + SLOTS) * TILES], i32)
        type_idx = y_sb[:, :, :].rearrange("p w d -> p (w d)")[:, 0:(chunks + SLOTS) * TILES].bitcast(i32)
        dst_f = sb("dst_f", [P, chunks * TILES])
        staged_src = sb("staged_src", [P, SLOTS, TILES], i32)
        staged_dst = sb("staged_dst", [P, SLOTS, TILES], i32)
        rows = sb("rows", [P, SLOTS, TILES, ROW])
        part_rows = rows[:, :, :, :].rearrange("p s t r -> p (s t r)").bitcast(bf16)\
            .rearrange("p (s t r) -> p s t r", s=SLOTS, t=TILES)
        shared = sb("shared", [P, SLOTS * TILES * D * 2 + SLOTS * EDGES + 2 * EDGES])
        def share(start, count):
            return shared[:, start:start + count]

        n_proj = SLOTS * TILES * D
        at_wide = n_proj
        at_proj = at_wide + SLOTS * EDGES
        at_scores = at_proj + n_proj
        attr = share(0, n_proj).rearrange("p (s t d) -> p s t d", s=SLOTS, t=TILES)
        dst_wide = share(at_wide, SLOTS * EDGES).bitcast(i32).rearrange("p (s e) -> p s e", s=SLOTS)
        dst_proj = share(at_proj, n_proj).rearrange("p (s t d) -> p s t d", s=SLOTS, t=TILES)
        scores = share(at_scores, EDGES)
        weights = share(at_scores + EDGES, EDGES)
        table_rows = share(at_proj, 2 * R_ATT * 2 * D).rearrange("p (k r d) -> p k r d", k=2, r=R_ATT)
        parts = shared[:, 0:W * PARTS * D // 2].bitcast(bf16).rearrange("p (w q d) -> p w q d", w=W, q=PARTS)
        onehot = sb("onehot", [P, TILES, P], bf16)
        att = sb("att", [P, 2, TILES])
        rescale_kept = sb("rescale_kept", [P, 1])
        degree = sb("degree", [P, W])
        node_max = sb("node_max", [P, W])
        step_max = sb("step_max", [P, 1])
        new_max = sb("new_max", [P, 1])
        neg_max = sb("neg_max", [P, 1])
        rescale = sb("rescale", [P, 1])
        stat = sb("stat", [P, W])
        stat2 = sb("stat2", [P, W])
        inv_sqrt_deg = sb("inv_sqrt_deg", [P, W])
        cat = sb("cat", [P, GROUP, 2 * D])
        cat_t = sb("cat_t", [P, GROUP * P])
        gates = sb("gates", [P, GROUP, 4 * D])
        hid = sb("hid", [P, GROUP, D])
        hid2 = sb("hid2", [P, GROUP, D])
        chunk_dst = shared[0:ROUNDS, 0:SLOTS * EDGES].bitcast(i32).rearrange("p (c e) -> p c e", c=SLOTS)
        bounds = sb("bounds", [ROUNDS, 2 * SLOTS], i32)
        bounds_row = sb("bounds_row", [1, ROUNDS * 2 * SLOTS], i32)
        lanes_i = sb("lanes_i", [P, P], i32)
        lanes = sb("lanes", [P, P])
        ids_i = sb("ids_i", [P, 2, W], i32)
        window_start = sb("window_start", [P, W])
        node_id = sb("node_id", [P, W])
        ident = sb("ident", [P, P])
        w1_sb = sb("w1_sb", [2 * D, D])
        w2_sb = sb("w2_sb", [2 * D, D])
        w8_sb = sb("w8_sb", [D, R_GRU * D])
        w10_sb = sb("w10_sb", [D, R_ATT * D])
        wg_sb = sb("wg_sb", [2 * D, 4 * D])
        wr_sb = sb("wr_sb", [2 * D, 2 * D])
        b1_sb = sb("b1_sb", [P, D])
        b2_sb = sb("b2_sb", [P, D])
        bg_sb = sb("bg_sb", [P, 4 * D])
        bh_sb = hid2[:, 0:3, :].rearrange("p g d -> p (g d)")

        turned_ps = pb("turned_ps", [P, 1024])
        prod_ps = pb("prod_ps", [P, 2048])
        sums_ps = pb("sums_ps", [P, D + 1])

        N_CONST = 14
        const_loaded = sem("const_loaded")
        x_loaded = sem("x_loaded")
        iota_done = sem("iota_done")
        setup_done = sem("setup_done")
        bounds_found = sem("bounds_found")
        bounds_saved = sem("bounds_saved")
        bounds_loaded = sem("bounds_loaded")
        dst_loaded = sem("dst_loaded")
        types_loaded = sem("types_loaded")
        types_wanted = sem("types_wanted")
        idx_ready = sem("idx_ready")
        var_ready = sem("var_ready")
        std_ready = sem("std_ready")
        rows_wanted = sem("rows_wanted")
        out_written = sem("out_written")
        dve_done = sem("dve_done")
        apart = {e: sem(f"apart_{e}") for e in ("sync", "pool", "act", "dve", "pe")}

        def stand_alone(engine, name):
            engine.sem_inc(apart[name], 1)

        class Chain:

            def __init__(self, eng):
                self.eng, self.base, self.n = eng, 0, 0

            def link(self, ins):
                self.n += 1
                ins.then_inc(dve_done, 1)
                self.eng.wait_ge(dve_done, self.base + self.n)

        def stage(name, names):
            return {n: sem(f"{name}_{n}") for n in names}

        SLOT = [f"{a}{k}" for a in ("gathered", "ring_free") for k in range(SLOTS)]
        PASS = ["table_ready", "written0", "written1", "staged", "onehot_ready", "sums_ready", "acc_added"]
        NODE = ["cat_ready", "turned", "copied", "multiplied", "taken"]
        TABLE = ["picked", "turned", "copied"] + [f"{a}{k}" for a in ("projected", "rows_ready", "rows_written")
                                                  for k in range(2)]
        plain_slots = stage("plain", SLOT)
        passes = [{"before": n * ROUNDS, **plain_slots, **stage(f"pass{n}", PASS if n < 5 else PASS[3:])}
                  for n in range(6)]
        sages = [stage(f"sage{n}", NODE) for n in range(2)]
        gru = stage("gru", NODE + ["squashed", "new_ready", "cand_ready"])
        final = stage("final", NODE)
        tab8 = stage("tab8", TABLE + [f"{a}{k}" for a in ("high", "rest", "mid") for k in range(2)])
        tab10 = stage("tab10", TABLE)
        attn = stage("attn", SLOT + [f"{a}{k}" for a in ("attr_loaded", "dst_loaded") for k in range(SLOTS)] +
                     ["staged", "summed", "squashed", "scaled", "score_ready", "spread", "far_ready", "masked",
                      "max_ready", "neg_ready", "kept", "rescaled", "exp_ready", "turned", "copied", "sums_ready", "acc_added"])

        def projected(k, R):
            return prod_ps[:, 2 * k * 512:2 * (k + 1) * 512].rearrange("p (b c) -> p b c", b=2)[:, :, 0:R * D // 2]\
                .rearrange("p b (r d) -> p b r d", d=D)

        def gates_rest(k):
            return (gates[:, :, :].rearrange("p g c -> p (g c)")[:, k * R_GRU * D:(k + 1) * R_GRU * D]
                    .rearrange("p (r d) -> p r d", d=D))

        block = ctx.enter_context(nc.Block())

        by_window = table.rearrange("(w p) (q d) -> p w q d", p=P, q=PARTS)
        HW = W // 2

        def load_bounds(eng, regs, i):
            eng.load(regs, bounds_row[0:1, bass.ds(i * 2 * SLOTS, 2 * SLOTS)])

        def windows(eng, regs, k):
            return eng.Fori(eng.snap(regs[2 * k], min_val=0, max_val=W - 1),
                            eng.snap(regs[2 * k + 1], min_val=1, max_val=W))

        def rounds(eng, one):
            with eng.Fori(0, ROUNDS - 1) as i:
                one(i, False)
            one(ROUNDS - 1, True)

        def att_rows(k):
            return table_rows[:, k, :, :]

        def part_table(k):
            return table_rows[:, k, :, :].rearrange("p r d -> p (r d)")[:, 0:R_GRU * PARTS * D // 2].bitcast(bf16)\
                .rearrange("p (r q d) -> p r q d", r=R_GRU, q=PARTS)

        @block.sync
        def _(sp):
            sp.dma_start(x_sb[:, :, :], x.rearrange("(w p) d -> p w d", p=P)).then_inc(x_loaded, 16)
            sp.dma_start(chunk_dst, dst_rows).then_inc(dst_loaded, 16)
            sp.dma_start(dst_idx[:, :], dst).then_inc(const_loaded, 16)
            sp.dma_start(src_idx[:, :], src).then_inc(const_loaded, 16)
            for to, of in ((ident, identity), (w1_sb, w_sage1), (w2_sb, w_sage2), (w8_sb, w_types8),
                           (w10_sb, w_types10), (wg_sb, w_gru), (wr_sb, w_res)):
                sp.dma_start(to[:, :], of).then_inc(const_loaded, 16)
            for to, of in ((b1_sb[:, :], b_sage1), (b2_sb[:, :], b_sage2), (bg_sb[:, 0:3 * D], b_ih),
                           (bh_sb, b_hh), (bg_sb[:, 3 * D:4 * D], b_hh[:, 2 * D:3 * D])):
                sp.dma_start(to, of.to_broadcast([P, of.shape[1]])).then_inc(const_loaded, 16)
            sp.wait_ge(bounds_found, 1)
            sp.dma_start(bounds_dram, bounds[:, :]).then_inc(bounds_saved, 16)
            sp.wait_ge(bounds_saved, 16)
            sp.dma_start(bounds_row[:, :], bounds_dram.rearrange("(o i) b -> o (i b)", o=1))\
              .then_inc(bounds_loaded, 16)

            for n in range(5):
                for b in range(2):
                    sp.wait_ge(passes[n]["table_ready"], b + 1)
                    sp.dma_start(by_window[:, b * HW:(b + 1) * HW, :, :], parts[:, b * HW:(b + 1) * HW, :, :])\
                      .then_inc(passes[n][f"written{b}"], 16)

            def write_table(s, to, R, ready, buffer):
                rows_of = to.rearrange("(w p r) d -> w p (r d)", p=P, r=R)
                with sp.Fori(0, W // 2) as j:
                    for k in range(2):
                        sp.wait_ge(s[f"rows_ready{k}"], ready * (j + 1))
                        sp.dma_start(rows_of[bass.ds(2 * j + k, 1), :, :].rearrange("o p f -> (o p) f"), buffer(k))\
                          .then_inc(s[f"rows_written{k}"], 16)

            sp.wait_ge(types_wanted, 1)
            sp.dma_start(type_idx, type8).then_inc(types_loaded, 16)
            write_table(tab8, table8, R_GRU, 1, lambda k: part_table(k).rearrange("p r q d -> p (r q d)"))
            sp.wait_ge(types_wanted, 2)
            sp.dma_start(type_idx, type10).then_inc(types_loaded, 16)
            sp.dma_start(src_idx[:, :], src).then_inc(types_loaded, 16)
            write_table(tab10, table10, R_ATT, 4, lambda k: att_rows(k).rearrange("p r d -> p (r d)"))

            def attention_inputs(i, k, first):
                if not first:
                    sp.wait_ge(attn[f"ring_free{k}"], i)
                sp.dma_start(attr[:, k, :, :],
                             edge_attr[bass.ds(SLOTS * i + k, 1), :, :, :].rearrange("o p t d -> (o p) t d"))\
                  .then_inc(attn[f"attr_loaded{k}"], 16)
                sp.dma_start(dst_wide[:, k, :],
                             dst_rows[bass.ds(i, 1), k, :].to_broadcast([P, EDGES]))\
                  .then_inc(attn[f"dst_loaded{k}"], 16)

            for k in range(SLOTS):
                attention_inputs(0, k, True)
            with sp.Fori(1, ROUNDS) as i:
                for k in range(SLOTS):
                    attention_inputs(i, k, False)

            sp.wait_ge(rows_wanted, 1)
            sp.dma_start(out.rearrange("(w p) d -> p w d", p=P), x_sb[:, :, :]).then_inc(out_written, 16)
            sp.wait_ge(out_written, 16)

        @block.gpsimd
        def _(pool):
            pool.iota(lanes_i[:, :], pattern=[[1, P]], base=0, channel_multiplier=0).then_inc(iota_done, 1)
            pool.iota(ids_i[:, 0, :], pattern=[[P, W]], base=0, channel_multiplier=0).then_inc(iota_done, 1)
            pool.iota(ids_i[:, 1, :], pattern=[[P, W]], base=0, channel_multiplier=1).then_inc(iota_done, 1)
            pool.memset(rows[:, :, :, 2 * D:ROW], 1.0).then_inc(iota_done, 1)
            pool.memset(part_rows[:, :, :, PARTS * D:PARTS * D + 1], 1.0).then_inc(iota_done, 1)

            def gather(k, t, from_, idx, to, s):
                pool.indirect_dma_start(out=to, out_offset=None, in_=from_,
                                        in_offset=bass.IndirectOffsetOnAxis(ap=idx[:, k, t:t + 1], axis=0))\
                    .then_inc(s[f"gathered{k}"], 16)

            def gather_pass(s, chunk):
                for k in range(SLOTS):
                    pool.wait_ge(s["staged"], k + 1)
                    chunk(k)
                with pool.Fori(1, ROUNDS) as i:
                    for k in range(SLOTS):
                        pool.wait_ge(s["staged"], SLOTS * i + k + 1)
                        pool.wait_ge(s[f"ring_free{k}"], s.get("before", 0) + i)
                        stand_alone(pool, "pool")
                        chunk(k)

            def plain_pass(s, from_):
                def chunk(k):
                    for t in range(TILES):
                        gather(k, t, from_, staged_src, part_rows[:, k, t, 0:PARTS * D], s)
                gather_pass(s, chunk)

            for n in range(5):
                for b in range(2):
                    pool.wait_ge(passes[n][f"written{b}"], 16)
                plain_pass(passes[n], table)
            for k in range(2):
                pool.wait_ge(tab8[f"rows_written{k}"], 16 * (W // 2))
            plain_pass(passes[5], table8)

            for k in range(2):
                pool.wait_ge(tab10[f"rows_written{k}"], 16 * (W // 2))
            halves = table10.rearrange("n (b d) -> (n b) d", b=2)

            def attention_chunk(k):
                for t in range(TILES):
                    gather(k, t, table10, staged_src, rows[:, k, t, 0:2 * D], attn)
                    gather(k, t, halves, staged_dst, dst_proj[:, k, t, :], attn)
            gather_pass(attn, attention_chunk)

        @block.scalar
        def _(act):
            def stage_indices(s, m, k, pairs):
                for to, of in pairs:
                    last = act.activation(to[:, k, :], of[:, bass.ds(m * TILES, TILES)], ACT.Copy)
                last.then_inc(s["staged"], 1)

            def plain_pass(s):
                pairs = [(staged_src, src_idx)]
                for k in range(SLOTS):
                    stage_indices(s, k, k, pairs)
                with act.Fori(0, ROUNDS) as i:
                    for k in range(SLOTS):
                        act.wait_ge(s[f"gathered{k}"], 16 * TILES * (s["before"] + i + 1))
                        stand_alone(act, "act")
                        stage_indices(s, SLOTS * (i + 1) + k, k, pairs)
                act.wait_ge(s["staged"], SLOTS * (ROUNDS + 1))

            def norm(n):
                act.wait_ge(var_ready, n)
                act.activation(stat2[:, :], stat[:, :], ACT.Sqrt).then_inc(std_ready, 1)

            def copy_turned(s, g):
                act.wait_ge(s["turned"], g + 1)
                act.activation(cat_t[:, :], turned_ps[:, 0:GROUP * P], ACT.Copy).then_inc(s["copied"], 1)

            def each_group(s):
                with act.Fori(0, NG) as g:
                    copy_turned(s, g)

            def pick(s, j):
                act.activation(cat[:, 0:2, 0:D], h_sb[:, bass.ds(2 * j, 2), :], ACT.Copy).then_inc(s["picked"], 1)

            def pair_loop(s, finish):
                def one(j, first, last):
                    act.wait_ge(s["turned"], j + 1)
                    act.activation(cat_t[0:D, 0:2 * P], turned_ps[0:D, 0:2 * P], ACT.Copy).then_inc(s["copied"], 1)
                    if not last:
                        pick(s, j + 1)
                    finish(j, first)
                pick(s, 0)
                one(0, True, False)
                with act.Fori(1, W // 2 - 1) as j:
                    one(j, False, False)
                one(W // 2 - 1, False, True)

            def tab8_finish(j, first):
                for k in range(2):
                    act.wait_ge(tab8[f"projected{k}"], j + 1)
                    if not first:
                        act.wait_ge(tab8[f"rows_written{k}"], 16 * j)
                    act.activation(part_table(k)[:, :, 0, :].rearrange("p (b r) d -> p b r d", b=2),
                                   projected(k, R_GRU), ACT.Copy).then_inc(tab8[f"high{k}"], 1)
                for k in range(2):
                    act.wait_ge(tab8[f"rest{k}"], j + 1)
                    act.activation(part_table(k)[:, :, 1, :], gates_rest(k), ACT.Copy)\
                       .then_inc(tab8[f"mid{k}"], 1)

            def tab10_finish(j, first):
                for k in range(2):
                    if not first:
                        act.wait_ge(tab10[f"rows_written{k}"], 16 * j)
                        stand_alone(act, "act")
                    act.activation(att_rows(k)[:, R_ATT // 2:, D:2 * D],
                                   h_sb[:, bass.ds(2 * j + k, 1), :].to_broadcast([P, R_ATT // 2, D]), ACT.Copy)\
                       .then_inc(tab10[f"rows_ready{k}"], 1)
                    act.wait_ge(tab10[f"projected{k}"], j + 1)
                    act.activation(att_rows(k)[:, R_ATT // 2:, 0:D], projected(k, R_ATT)[:, 1, :, :], ACT.Copy)\
                       .then_inc(tab10[f"rows_ready{k}"], 1)

            act.wait_ge(const_loaded, 16 * N_CONST)
            norm(1)
            plain_pass(passes[0])
            each_group(sages[0])
            plain_pass(passes[1])
            each_group(sages[1])
            norm(2)
            norm(3)
            for n in (2, 3, 4):
                plain_pass(passes[n])
            norm(4)
            act.wait_ge(idx_ready, 1)
            pair_loop(tab8, tab8_finish)
            plain_pass(passes[5])

            def gru_one(g, last):
                act.wait_ge(gru["taken"], g + 2)
                act.activation(gates[:, :, 0:2 * D], gates[:, :, 0:2 * D], ACT.Tanh, scale=0.5)\
                   .then_inc(gru["squashed"], 1)
                if not last:
                    copy_turned(gru, g + 1)
                act.wait_ge(gru["cand_ready"], g + 1)
                act.activation(hid[:, :, :], hid[:, :, :], ACT.Tanh).then_inc(gru["new_ready"], 1)

            copy_turned(gru, 0)
            with act.Fori(0, NG - 1) as g:
                gru_one(g, False)
            gru_one(NG - 1, True)
            norm(5)
            act.wait_ge(idx_ready, 2)
            pair_loop(tab10, tab10_finish)

            pairs = [(staged_src, src_idx), (staged_dst, dst_idx)]
            for k in range(SLOTS):
                stage_indices(attn, k, k, pairs)
            bound = [act.alloc_register(f"act_bound{k}") for k in range(2 * SLOTS)]
            steps = act.alloc_register("act_steps")
            act.reg_mov(steps, 0)

            def prepare(i, k, m):
                act.wait_ge(attn[f"gathered{k}"], 32 * TILES * (i + 1))
                stand_alone(act, "act")
                stage_indices(attn, m + SLOTS, k, pairs)
                act.wait_ge(attn["summed"], m + 1)
                act.activation(dst_proj[:, k, :, :], dst_proj[:, k, :, :], ACT.Tanh).then_inc(attn["squashed"], 1)

            def attention_round(i, last):
                load_bounds(act, bound, i)
                for k in range(SLOTS):
                    if not (last and k == SLOTS - 1):
                        prepare(i + (k + 1) // SLOTS, (k + 1) % SLOTS, SLOTS * i + k + 1)
                    with windows(act, bound, k) as n:
                        s = act.snap(steps)
                        act.wait_ge(attn["neg_ready"], s + 1)
                        stand_alone(act, "act")
                        act.activation(rescale[:, :], node_max[:, bass.ds(n, 1)], ACT.Exp, bias=neg_max[:, 0:1])\
                           .then_inc(attn["rescaled"], 1)
                        for h in range(2):
                            part = scores[:, h * 4 * P:(h + 1) * 4 * P]
                            act.activation(part, part, ACT.Exp, bias=neg_max[:, 0:1]).then_inc(attn["exp_ready"], 1)
                            if h == 0:
                                act.wait_ge(attn["rescaled"], s + 1)
                                stand_alone(act, "act")
                                act.activation(node_max[:, bass.ds(n, 1)], new_max[:, :], ACT.Copy)
                        for h in range(2):
                            act.wait_ge(attn["turned"], 2 * s + h + 2)
                            act.activation(weights[:, h * 4 * P:(h + 1) * 4 * P],
                                           turned_ps[:, h * 4 * P:(h + 1) * 4 * P], ACT.Copy)\
                               .then_inc(attn["copied"], 1)
                        act.reg_add(steps, steps, 1)
            prepare(0, 0, 0)
            rounds(act, attention_round)
            each_group(final)

        @block.tensor
        def _(pe):
            pe.wait_ge(const_loaded, 16 * N_CONST)
            pe.wait_ge(iota_done, 5)
            pe.wait_ge(bounds_loaded, 16)
            bound = [pe.alloc_register(f"pe_bound{k}") for k in range(2 * SLOTS)]
            steps = pe.alloc_register("pe_steps")

            def plain_pass(s):
                pe.reg_mov(steps, 0)
                with pe.Fori(0, ROUNDS) as i:
                    load_bounds(pe, bound, i)
                    for k in range(SLOTS):
                        pe.wait_ge(s[f"gathered{k}"], 16 * TILES * (s["before"] + i + 1))
                        stand_alone(pe, "pe")
                        with windows(pe, bound, k) as _n:
                            st = pe.snap(steps)
                            for t in range(TILES):
                                if t % HALF == 0:
                                    pe.wait_ge(s["onehot_ready"], 2 * st + t // HALF + 1)
                                for q in (2, 1, 0):
                                    n = D + 1 if q == 2 else D
                                    last = pe.matmul(sums_ps[:, 0:n], onehot[:, t, :],
                                                     part_rows[:, k, t, q * D:q * D + n],
                                                     start=(t == 0 and q == 2), stop=(t == TILES - 1 and q == 0))
                            last.then_inc(s["sums_ready"], 1)
                            pe.reg_add(steps, steps, 1)
                        pe.drain().then_inc(s[f"ring_free{k}"], 1)

            def turn(s, g):
                pe.wait_ge(s["cat_ready"], g + 1)
                for k in range(GROUP):
                    last = pe.transpose(turned_ps[:, k * P:(k + 1) * P], cat[:, k, :], ident[:, :])
                last.then_inc(s["turned"], 1)

            def node_stage(s, w, cols):
                per_bank = 512 // cols

                def one(g, last_group):
                    pe.wait_ge(s["copied"], g + 1)
                    pe.wait_ge(s["taken"], g + 1)
                    for k in range(GROUP):
                        c = (k // per_bank) * 512 + (k % per_bank) * cols
                        last = pe.matmul(prod_ps[:, c:c + cols], cat_t[:, k * P:(k + 1) * P], w[:, :],
                                         start=True, stop=True)
                    last.then_inc(s["multiplied"], 1)
                    if not last_group:
                        turn(s, g + 1)
                turn(s, 0)
                with pe.Fori(0, NG - 1) as g:
                    one(g, False)
                one(NG - 1, True)

            def make_table(s, w, R, ready):
                half = R * D // 2

                def turn_pair(j):
                    pe.wait_ge(s["picked"], j + 1)
                    stand_alone(pe, "pe")
                    for k in range(2):
                        last = pe.transpose(turned_ps[0:D, k * P:(k + 1) * P], cat[:, k, 0:D], ident[:, :])
                    last.then_inc(s["turned"], 1)

                def one(j, first, last_pair):
                    pe.wait_ge(s["copied"], j + 1)
                    for k in range(2):
                        if not first:
                            pe.wait_ge(s[f"rows_ready{k}"], ready * j)
                        for b in range(2):
                            c = (2 * k + b) * 512
                            last = pe.matmul(prod_ps[:, c:c + half], cat_t[0:D, k * P:(k + 1) * P],
                                             w[:, b * half:(b + 1) * half], start=True, stop=True)
                        last.then_inc(s[f"projected{k}"], 1)
                    if not last_pair:
                        turn_pair(j + 1)
                turn_pair(0)
                one(0, True, False)
                with pe.Fori(1, W // 2 - 1) as j:
                    one(j, False, False)
                one(W // 2 - 1, False, True)

            plain_pass(passes[0])
            node_stage(sages[0], w1_sb, D)
            plain_pass(passes[1])
            node_stage(sages[1], w2_sb, D)
            for n in (2, 3, 4):
                plain_pass(passes[n])
            make_table(tab8, w8_sb, R_GRU, 1)
            plain_pass(passes[5])
            node_stage(gru, wg_sb, 4 * D)
            make_table(tab10, w10_sb, R_ATT, 4)

            pe.reg_mov(steps, 0)

            def spread(m, k):
                pe.wait_ge(attn["score_ready"], m + 1)
                for t in range(TILES):
                    c = (k % 2) * EDGES + t * P
                    last = pe.matmul(prod_ps[:, c:c + P], att[:, k % 2, t:t + 1].to_broadcast([P, P]),
                                     ident[:, :], start=True, stop=True)
                last.then_inc(attn["spread"], 1)

            def attention_round(i, last_round):
                load_bounds(pe, bound, i)
                for k in range(SLOTS):
                    if not (last_round and k == SLOTS - 1):
                        spread(SLOTS * i + k + 1, k + 1)
                    with windows(pe, bound, k) as _n:
                        st = pe.snap(steps)
                        for h in range(2):
                            pe.wait_ge(attn["exp_ready"], 2 * st + h + 1)
                            for t in range(h * HALF, (h + 1) * HALF):
                                last = pe.transpose(turned_ps[:, t * P:(t + 1) * P], scores[:, t * P:(t + 1) * P],
                                                    ident[:, :])
                            last.then_inc(attn["turned"], 1)
                        pe.wait_ge(attn["acc_added"], st + 2)
                        for t in range(TILES):
                            if t % HALF == 0:
                                pe.wait_ge(attn["copied"], 2 * st + t // HALF + 1)
                            last = pe.matmul(sums_ps[:, :], weights[:, t * P:(t + 1) * P], rows[:, k, t, D:ROW],
                                             start=(t == 0), stop=(t == TILES - 1))
                        last.then_inc(attn["sums_ready"], 1)
                        pe.reg_add(steps, steps, 1)
                    pe.drain().then_inc(attn[f"ring_free{k}"], 1)
            pe.sem_inc(attn["turned"], 1)
            pe.sem_inc(attn["sums_ready"], 1)
            spread(0, 0)
            rounds(pe, attention_round)
            node_stage(final, wr_sb, 2 * D)

        @block.vector
        def _(dve):
            chain = Chain(dve)
            link = chain.link
            bound = [dve.alloc_register(f"dve_bound{k}") for k in range(2 * SLOTS)]
            steps = dve.alloc_register("dve_steps")
            last_window = dve.alloc_register("dve_last_window")

            def per_node(v):
                return v.unsqueeze(2).to_broadcast([P, v.shape[1], D])

            def layer_norm(n):
                link(dve.tensor_reduce(stat[:, :], x_sb[:, :, :], AX.X, ALU.add))
                link(dve.tensor_scalar(stat[:, :], stat[:, :], 1.0 / D, None, ALU.mult))
                link(dve.tensor_tensor(y_sb[:, :, :], x_sb[:, :, :], per_node(stat[:, :]), ALU.subtract))
                link(dve.tensor_tensor(h_sb[:, :, :], y_sb[:, :, :], y_sb[:, :, :], ALU.mult))
                link(dve.tensor_reduce(stat[:, :], h_sb[:, :, :], AX.X, ALU.add))
                dve.tensor_scalar(stat[:, :], stat[:, :], 1.0 / D, EPS, ALU.mult, ALU.add).then_inc(var_ready, 1)
                dve.wait_ge(std_ready, n)
                link(dve.reciprocal(stat[:, :], stat2[:, :]))
                link(dve.scalar_tensor_tensor(h_sb[:, :, :], y_sb[:, :, :], 0.0, per_node(stat[:, :]),
                                              ALU.max, ALU.mult))

            def save_table(s, v, rest):
                for b in range(2):
                    at = slice(b * HW, (b + 1) * HW)
                    link(dve.tensor_copy(parts[:, at, 0, :], v[:, at, :]))
                    link(dve.tensor_tensor(rest[:, at, :], v[:, at, :], parts[:, at, 0, :], ALU.subtract))
                    link(dve.tensor_copy(parts[:, at, 1, :], rest[:, at, :]))
                    dve.tensor_tensor(parts[:, at, 2, :], rest[:, at, :], parts[:, at, 1, :], ALU.subtract)\
                       .then_inc(s["table_ready"], 1)

            def plain_pass(s):
                dve.memset(acc[:, :, :], 0.0).then_inc(s["acc_added"], 1)
                dve.reg_mov(steps, 0)
                with dve.Fori(0, ROUNDS) as i:
                    load_bounds(dve, bound, i)
                    for k in range(SLOTS):
                        with windows(dve, bound, k) as n:
                            st = dve.snap(steps)
                            dve.wait_ge(s["acc_added"], st + 1)
                            for h in range(2):
                                here = dst_f[:, bass.ds((SLOTS * i + k) * TILES + h * HALF, HALF)].unsqueeze(2)\
                                    .to_broadcast([P, HALF, P])
                                dve.scalar_tensor_tensor(onehot[:, h * HALF:(h + 1) * HALF, :], here,
                                                         window_start[:, bass.ds(n, 1)],
                                                         lanes[:, :].unsqueeze(1).to_broadcast([P, HALF, P]),
                                                         ALU.subtract, ALU.is_equal).then_inc(s["onehot_ready"], 1)
                            dve.wait_ge(s["sums_ready"], st + 1)
                            at = acc[:, bass.ds(n, 1), :].rearrange("p o d -> p (o d)")
                            dve.tensor_tensor(at, at, sums_ps[:, :], ALU.add).then_inc(s["acc_added"], 1)
                            dve.reg_add(steps, steps, 1)
                dve.wait_ge(s["acc_added"], dve.snap(steps) + 1)
                stand_alone(dve, "dve")

            def group(buf, g):
                return buf[:, bass.ds(g * GROUP, GROUP), 0:D]

            def each_group(s, fill, finish, links):
                def one(g, last):
                    if not last:
                        dve.wait_ge(s["turned"], g + 1)
                        stand_alone(dve, "dve")
                        fill(g + 1)
                    dve.wait_ge(s["multiplied"], g + 1)
                    finish(g)
                dve.sem_inc(s["taken"], 1)
                fill(0)
                start = chain.n
                with dve.Fori(0, NG - 1) as g:
                    chain.base, chain.n = g * links + start, 0
                    one(g, False)
                    assert chain.n == links
                chain.base, chain.n = 0, start + (NG - 1) * links
                one(NG - 1, True)

            dve.wait_ge(x_loaded, 16)
            layer_norm(1)
            dve.wait_ge(dst_loaded, 16)
            lohi = bounds[:, :].rearrange("p (c b) -> p c b", b=2)
            link(dve.tensor_reduce(lohi[:, :, 0], chunk_dst, AX.X, ALU.min))
            link(dve.tensor_reduce(lohi[:, :, 1], chunk_dst, AX.X, ALU.max))
            link(dve.tensor_scalar(bounds[:, :], bounds[:, :], 7, None, ALU.arith_shift_right))
            dve.tensor_scalar(lohi[:, :, 1], lohi[:, :, 1], 1.0, None, ALU.add).then_inc(bounds_found, 1)
            save_table(passes[0], h_sb, y_sb)
            dve.wait_ge(iota_done, 5)
            link(dve.tensor_copy(lanes[:, :], lanes_i[:, :]))
            link(dve.tensor_copy(window_start[:, :], ids_i[:, 0, :]))
            link(dve.tensor_copy(node_id[:, :], ids_i[:, 1, :]))
            dve.wait_ge(const_loaded, 16 * N_CONST)
            link(dve.tensor_copy(dst_f[:, :], dst_idx[:, 0:chunks * TILES]))
            link(dve.tensor_tensor(bg_sb[:, 0:2 * D], bg_sb[:, 0:2 * D], bh_sb[:, 0:2 * D], ALU.add))
            dve.wait_ge(bounds_loaded, 16)

            def sage(s, bias, put):
                link(dve.tensor_scalar(stat[:, :], acc[:, :, D], 1.0, None, ALU.max))
                link(dve.reciprocal(stat2[:, :], stat[:, :]))

                def fill(g):
                    dve.tensor_tensor(cat[:, :, 0:D], group(acc, g),
                                      stat2[:, bass.ds(g * GROUP, GROUP)].unsqueeze(2)
                                      .to_broadcast([P, GROUP, D]), ALU.mult)
                    dve.tensor_copy(cat[:, :, D:2 * D], group(h_sb, g)).then_inc(s["cat_ready"], 1)

                def finish(g):
                    dve.tensor_tensor(hid[:, :, :], prod_ps[:, 0:GROUP * D].rearrange("p (k d) -> p k d", d=D),
                                      bias[:, :].unsqueeze(1).to_broadcast([P, GROUP, D]), ALU.add)\
                       .then_inc(s["taken"], 1)
                    dve.wait_ge(s["taken"], g + 2)
                    stand_alone(dve, "dve")
                    link(put(g))
                each_group(s, fill, finish, 1)

            plain_pass(passes[0])
            sage(sages[0], b1_sb,
                 lambda g: dve.tensor_scalar(group(h_sb, g), hid[:, :, :], 0.0, None, ALU.max))
            save_table(passes[1], h_sb, y_sb)
            plain_pass(passes[1])
            sage(sages[1], b2_sb,
                 lambda g: dve.scalar_tensor_tensor(group(x_sb, g), hid[:, :, :], 0.0, group(x_sb, g),
                                                    ALU.max, ALU.add))

            layer_norm(2)
            link(dve.tensor_scalar(inv_sqrt_deg[:, :], acc[:, :, D], 1.0, None, ALU.min))
            dve.tensor_scalar(stat[:, :], acc[:, :, D], 1.0, None, ALU.max).then_inc(var_ready, 1)
            dve.wait_ge(std_ready, 3)
            link(dve.reciprocal(stat[:, :], stat2[:, :]))
            link(dve.tensor_tensor(inv_sqrt_deg[:, :], inv_sqrt_deg[:, :], stat[:, :], ALU.mult))
            for n in (2, 3, 4):
                link(dve.tensor_tensor(y_sb[:, :, :], h_sb[:, :, :], per_node(inv_sqrt_deg[:, :]), ALU.mult))
                save_table(passes[n], y_sb, y_sb)
                link(dve.scalar_tensor_tensor(x_sb[:, :, :], h_sb[:, :, :], 0.25, x_sb[:, :, :], ALU.mult, ALU.add))
                plain_pass(passes[n])
                link(dve.tensor_tensor(h_sb[:, :, :], acc[:, :, 0:D], per_node(inv_sqrt_deg[:, :]), ALU.mult))
            link(dve.scalar_tensor_tensor(x_sb[:, :, :], h_sb[:, :, :], 0.25, x_sb[:, :, :], ALU.mult, ALU.add))

            def pair_loop(one):
                one(0, True)
                with dve.Fori(1, W // 2) as j:
                    one(j, False)

            layer_norm(4)
            dve.sem_inc(types_wanted, 1)
            dve.wait_ge(types_loaded, 16)
            link(dve.tensor_scalar(src_idx[:, :], src_idx[:, :], float(R_GRU), None, ALU.mult))
            dve.tensor_tensor(src_idx[:, :], src_idx[:, :], type_idx, ALU.add).then_inc(idx_ready, 1)

            def tab8_one(j, first):
                for k in range(2):
                    dve.wait_ge(tab8[f"high{k}"], j + 1)
                    dve.tensor_tensor(gates_rest(k).rearrange("p (b r) d -> p b r d", b=2), projected(k, R_GRU),
                                      part_table(k)[:, :, 0, :].rearrange("p (b r) d -> p b r d", b=2),
                                      ALU.subtract).then_inc(tab8[f"rest{k}"], 1)
                for k in range(2):
                    dve.wait_ge(tab8[f"mid{k}"], j + 1)
                    dve.tensor_tensor(part_table(k)[:, :, 2, :], gates_rest(k), part_table(k)[:, :, 1, :],
                                      ALU.subtract).then_inc(tab8[f"rows_ready{k}"], 1)
            pair_loop(tab8_one)
            plain_pass(passes[5])

            def gru_fill(g):
                dve.tensor_copy(cat[:, :, 0:D], group(acc, g))
                dve.tensor_copy(cat[:, :, D:2 * D], group(h_sb, g)).then_inc(gru["cat_ready"], 1)

            def gru_finish(g):
                dve.tensor_tensor(gates[:, :, :], prod_ps[:, 0:GROUP * 4 * D].rearrange("p (k c) -> p k c", c=4 * D),
                                  bg_sb[:, :].unsqueeze(1).to_broadcast([P, GROUP, 4 * D]), ALU.add)\
                   .then_inc(gru["taken"], 1)
                dve.wait_ge(gru["squashed"], g + 1)
                link(dve.scalar_tensor_tensor(hid[:, :, :], gates[:, :, 0:D], 1.0, gates[:, :, 3 * D:4 * D],
                                              ALU.add, ALU.mult))
                dve.scalar_tensor_tensor(hid[:, :, :], hid[:, :, :], 0.5, gates[:, :, 2 * D:3 * D],
                                         ALU.mult, ALU.add).then_inc(gru["cand_ready"], 1)
                dve.wait_ge(gru["new_ready"], g + 1)
                link(dve.tensor_tensor(hid2[:, :, :], group(h_sb, g), hid[:, :, :], ALU.subtract))
                link(dve.scalar_tensor_tensor(hid2[:, :, :], gates[:, :, D:2 * D], 1.0, hid2[:, :, :],
                                              ALU.add, ALU.mult))
                link(dve.scalar_tensor_tensor(hid2[:, :, :], hid2[:, :, :], 0.5, hid[:, :, :], ALU.mult, ALU.add))
                link(dve.tensor_tensor(group(x_sb, g), group(x_sb, g), hid2[:, :, :], ALU.add))
            each_group(gru, gru_fill, gru_finish, 5)

            layer_norm(5)
            dve.sem_inc(types_wanted, 1)
            dve.wait_ge(types_loaded, 16 * 3)
            for idx in (src_idx, dst_idx):
                link(dve.tensor_scalar(idx[:, :], idx[:, :], float(R_ATT), None, ALU.mult))
                link(dve.tensor_tensor(idx[:, :], idx[:, :], type_idx, ALU.add))
            dve.tensor_scalar(dst_idx[:, :], dst_idx[:, :], 2.0, None, ALU.mult).then_inc(idx_ready, 1)

            def tab10_one(j, first):
                for k in range(2):
                    if not first:
                        dve.wait_ge(tab10[f"rows_written{k}"], 16 * j)
                        stand_alone(dve, "dve")
                    dve.tensor_copy(att_rows(k)[:, 0:R_ATT // 2, D:2 * D],
                                    h_sb[:, bass.ds(2 * j + k, 1), :].to_broadcast([P, R_ATT // 2, D]))\
                       .then_inc(tab10[f"rows_ready{k}"], 1)
                    dve.wait_ge(tab10[f"projected{k}"], j + 1)
                    dve.tensor_copy(att_rows(k)[:, 0:R_ATT // 2, 0:D], projected(k, R_ATT)[:, 0, :, :])\
                       .then_inc(tab10[f"rows_ready{k}"], 1)
            pair_loop(tab10_one)

            link(dve.memset(node_max[:, :], LOW))
            link(dve.memset(sums_ps[:, :], 0.0))
            link(dve.memset(rescale[:, :], 1.0))
            dve.memset(acc[:, :, :], 0.0).then_inc(attn["acc_added"], 1)
            dve.reg_mov(steps, 0)
            dve.reg_mov(last_window, 0)

            def prepare(i, k, m):
                proj = dst_proj[:, k, :, :]
                dve.wait_ge(attn[f"gathered{k}"], 32 * TILES * (i + 1))
                dve.wait_ge(attn[f"attr_loaded{k}"], 16 * (i + 1))
                dve.tensor_tensor(proj, proj, attr[:, k, :, :], ALU.add).then_inc(attn["summed"], 1)
                dve.wait_ge(attn["squashed"], m + 1)
                dve.tensor_tensor(proj, proj, rows[:, k, :, 0:D], ALU.mult).then_inc(attn["scaled"], 1)
                dve.wait_ge(attn["scaled"], m + 1)
                dve.tensor_reduce(att[:, k % 2, :], proj, AX.X, ALU.add).then_inc(attn["score_ready"], 1)

            def add_sums(count):
                dve.wait_ge(attn["sums_ready"], count)
                at = acc[:, bass.ds(dve.snap(last_window, min_val=0, max_val=W - 1), 1), :]\
                    .rearrange("p o d -> p (o d)")
                dve.scalar_tensor_tensor(at, at, rescale_kept[:, 0:1], sums_ps[:, :], ALU.mult, ALU.add)\
                   .then_inc(attn["acc_added"], 1)

            def attention_round(i, last):
                load_bounds(dve, bound, i)
                for k in range(SLOTS):
                    m = SLOTS * i + k
                    if not (last and k == SLOTS - 1):
                        prepare(i + (k + 1) // SLOTS, (k + 1) % SLOTS, m + 1)
                    dve.wait_ge(attn["spread"], m + 1)
                    dve.wait_ge(attn[f"dst_loaded{k}"], 16 * (i + 1))
                    stand_alone(dve, "dve")
                    with windows(dve, bound, k) as n:
                        st = dve.snap(steps)
                        dve.wait_ge(attn["turned"], 2 * st + 1)
                        stand_alone(dve, "dve")
                        dve.tensor_scalar(scores, dst_wide[:, k, :], node_id[:, bass.ds(n, 1)], FAR,
                                          ALU.not_equal, ALU.mult).then_inc(attn["far_ready"], 1)
                        dve.wait_ge(attn["acc_added"], st + 1)
                        stand_alone(dve, "dve")
                        dve.tensor_copy(rescale_kept[:, :], rescale[:, :]).then_inc(attn["kept"], 1)
                        dve.wait_ge(attn["far_ready"], st + 1)
                        stand_alone(dve, "dve")
                        c = (k % 2) * EDGES
                        dve.tensor_tensor_reduce(out=scores, in0=scores, in1=prod_ps[:, c:c + EDGES],
                                                 scale=1.0, scalar=FAR, op0=ALU.add, op1=ALU.max,
                                                 accum_out=step_max[:, :]).then_inc(attn["masked"], 1)
                        dve.wait_ge(attn["masked"], st + 1)
                        dve.tensor_tensor(new_max[:, :], step_max[:, :], node_max[:, bass.ds(n, 1)], ALU.max)\
                           .then_inc(attn["max_ready"], 1)
                        dve.wait_ge(attn["max_ready"], st + 1)
                        dve.tensor_scalar(neg_max[:, :], new_max[:, :], -1.0, None, ALU.mult)\
                           .then_inc(attn["neg_ready"], 1)
                        dve.wait_ge(attn["kept"], st + 1)
                        add_sums(st + 1)
                        dve.reg_mov(last_window, n)
                        dve.reg_add(steps, steps, 1)
            prepare(0, 0, 0)
            rounds(dve, attention_round)
            dve.wait_ge(attn["sums_ready"], dve.snap(steps) + 1)
            dve.wait_ge(attn["acc_added"], dve.snap(steps) + 1)
            stand_alone(dve, "dve")
            link(dve.tensor_copy(rescale_kept[:, :], rescale[:, :]))
            add_sums(dve.snap(steps) + 1)
            dve.wait_ge(attn["acc_added"], dve.snap(steps) + 2)
            stand_alone(dve, "dve")
            link(dve.tensor_scalar(stat[:, :], acc[:, :, D], 1.0e-30, None, ALU.max))
            link(dve.reciprocal(stat2[:, :], stat[:, :]))
            link(dve.tensor_tensor(y_sb[:, :, :], acc[:, :, 0:D], per_node(stat2[:, :]), ALU.mult))

            def final_fill(g):
                dve.tensor_tensor(cat[:, :, 0:D], group(y_sb, g), group(h_sb, g), ALU.add)
                dve.tensor_tensor(cat[:, :, D:2 * D], group(y_sb, g), group(h_sb, g), ALU.mult)\
                   .then_inc(final["cat_ready"], 1)

            def final_finish(g):
                both = gates[:, :, 0:2 * D]
                dve.tensor_copy(both, prod_ps[:, 0:GROUP * 2 * D].rearrange("p (k c) -> p k c", c=2 * D))\
                   .then_inc(final["taken"], 1)
                dve.wait_ge(final["taken"], g + 2)
                link(dve.scalar_tensor_tensor(both, both, SLOPE, both, ALU.mult, ALU.max))
                link(dve.tensor_tensor(group(x_sb, g), group(x_sb, g), gates[:, :, 0:D], ALU.add))
                link(dve.tensor_tensor(group(x_sb, g), group(x_sb, g), gates[:, :, D:2 * D], ALU.add))
            each_group(final, final_fill, final_finish, 3)
            dve.sem_inc(rows_wanted, 1)


def kernel(**inputs):
    import numpy as np
    import concourse.bacc as bacc
    from concourse.bass_utils import run_bass_kernel_spmd

    a = {k: np.asarray(v) for k, v in inputs.items()}
    n_nodes, n_edges = a["x"].shape[0], a["src"].shape[0]
    tile_group = P * GROUP * 2
    nodes = -(-n_nodes // tile_group) * tile_group
    edges = P * TILES
    rounds = -(-n_edges // (SLOTS * edges))
    padded = rounds * SLOTS * edges
    tiles = padded // P

    def edge_list(v, fill):
        e = np.full([padded], fill, v.dtype)
        e[:n_edges] = v
        cols = np.zeros([P, tiles + SLOTS * TILES], v.dtype)
        cols[:, :tiles] = e.reshape(tiles, P).T
        return e, cols

    x = np.zeros([nodes, D], a["x"].dtype)
    x[:n_nodes] = a["x"]
    dst_flat, dst = edge_list(a["dst"], nodes - 1)
    attr = np.zeros([padded, D], a["edge_attr_64"].dtype)
    attr[:n_edges] = a["edge_attr_64"]
    T = lambda name: np.ascontiguousarray(a[name].T)
    w_ih, w_hh = T("L2_gnn_w_ih"), T("L2_gnn_w_hh")
    w_gru = np.zeros([2 * D, 4 * D], w_ih.dtype)
    w_gru[:D, :3 * D] = w_ih
    w_gru[D:, :2 * D] = w_hh[:, :2 * D]
    w_gru[D:, 3 * D:] = w_hh[:, 2 * D:]
    w_res = np.zeros([2 * D, 2 * D], w_ih.dtype)
    w_res[:D, :D] = T("L3_gnn_res_fc_w")
    w_res[D:, D:] = T("L3_gnn_res_fc2_w")
    arrays = {
        "x": x,
        "src": edge_list(a["src"], 0)[1],
        "dst": dst,
        "dst_rows": dst_flat.reshape(rounds, SLOTS, edges),
        "type8": edge_list(a["edge_type_8"], 0)[1],
        "type10": edge_list(a["edge_type_10"], 0)[1],
        "edge_attr": np.ascontiguousarray(attr.reshape(rounds * SLOTS, TILES, P, D).transpose(0, 2, 1, 3)),
        "w_sage1": np.concatenate([T("L0_gnn_W_l1"), T("L0_gnn_W_r1")]),
        "w_sage2": np.concatenate([T("L0_gnn_W_l2"), T("L0_gnn_W_r2")]),
        "b_sage1": a["L0_gnn_b1"][None, :],
        "b_sage2": a["L0_gnn_b2"][None, :],
        "w_types8": np.ascontiguousarray(a["L2_gnn_edge_matrix"].reshape(R_GRU, D, D).transpose(2, 0, 1)
                                         .reshape(D, R_GRU * D)),
        "w_gru": w_gru,
        "b_ih": a["L2_gnn_b_ih"][None, :],
        "b_hh": a["L2_gnn_b_hh"][None, :],
        "w_types10": np.ascontiguousarray(a["L3_gnn_relation_weight"].transpose(1, 0, 2).reshape(D, R_ATT * D)),
        "w_res": w_res,
        "identity": np.eye(P, dtype=np.float32),
    }
    nc = bacc.Bacc("TRN2", target_bir_lowering=False, num_devices=1)
    args = {n: nc.dram_tensor(f"in_{n}", v.shape, mybir.dt.from_np(v.dtype), kind="ExternalInput").ap()
            for n, v in arrays.items()}
    out = nc.dram_tensor("out", [nodes, D], mybir.dt.float32, kind="ExternalOutput").ap()
    build(nc, out=out, **args)
    r = run_bass_kernel_spmd(nc, [{f"in_{n}": v for n, v in arrays.items()}], core_ids=[0])
    return r.results[0]["out"][:n_nodes]
```

```python
import concourse.bass as bass
import concourse.mybir as mybir
from contextlib import ExitStack

P = 128
D = 64
TILES = 8
GROUP = 7
R_GRU = 8
R_ATT = 10
SLOTS = 4
HALF = TILES // 2
PARTS = 3
ROW = 2 * D + 1
EPS = 1e-5
SLOPE = 0.01
FAR = -3.0e38
LOW = -1.0e30


def build(nc, x, src, dst, dst_rows, type8, type10, edge_attr, w_sage1, w_sage2, b_sage1, b_sage2,
          w_types8, w_gru, b_ih, b_hh, w_types10, w_res, identity, out):
    fp32, i32, bf16 = mybir.dt.float32, mybir.dt.int32, mybir.dt.bfloat16
    ALU, ACT, AX = mybir.AluOpType, mybir.ActivationFunctionType, mybir.AxisListType
    W = x.shape[1]
    nodes = W * P
    NG = W // GROUP
    BATCH = 2 * GROUP
    B = W // BATCH
    ROUNDS = dst_rows.shape[0]
    chunks = ROUNDS * SLOTS
    EDGES = TILES * P
    IDX = (chunks + SLOTS) * TILES

    table = nc.dram_tensor("node_table", [nodes, PARTS * D], bf16).ap()
    table8 = nc.dram_tensor("type_table8", [nodes * R_GRU, PARTS * D], bf16).ap()
    table10 = nc.dram_tensor("type_table10", [nodes * R_ATT, 2 * D], fp32).ap()
    bounds_dram = nc.dram_tensor("bounds_dram", [ROUNDS, 2 * SLOTS], i32).ap()

    ctx = ExitStack()
    with ctx:
        def sb(name, shape, dt=fp32):
            return ctx.enter_context(nc.sbuf_tensor(name, shape, dt))

        def pb(name, shape):
            return ctx.enter_context(nc.psum_tensor(name, shape, fp32))

        def sem(name):
            return ctx.enter_context(nc.semaphore(name))

        x_sb = sb("x_sb", [P, W, D])
        h_sb = sb("h_sb", [P, W, D])
        y_sb = sb("y_sb", [P, W, D])
        acc = sb("acc", [P, W, D + 1])
        src_idx = sb("src_idx", [P, IDX], i32)
        dst_idx = sb("dst_idx", [P, IDX], i32)
        type_idx = y_sb[:, :, :].rearrange("p w d -> p (w d)")[:, 0:IDX].bitcast(i32)
        dst_f = sb("dst_f", [P, chunks * TILES])
        staged_src = sb("staged_src", [P, SLOTS, TILES], i32)
        staged_dst = sb("staged_dst", [P, SLOTS, TILES], i32)
        rows = sb("rows", [P, SLOTS, TILES, ROW])
        part_rows = rows[:, :, :, :].rearrange("p s t r -> p (s t r)").bitcast(bf16)\
            .rearrange("p (s t r) -> p s t r", s=SLOTS, t=TILES)
        shared = sb("shared", [P, SLOTS * TILES * D * 2 + SLOTS * EDGES + 2 * EDGES])

        def share(start, count):
            return shared[:, start:start + count]

        n_proj = SLOTS * TILES * D
        at_wide = n_proj
        at_proj = at_wide + SLOTS * EDGES
        at_scores = at_proj + n_proj
        attr = share(0, n_proj).rearrange("p (s t d) -> p s t d", s=SLOTS, t=TILES)
        dst_wide = share(at_wide, SLOTS * EDGES).bitcast(i32).rearrange("p (s e) -> p s e", s=SLOTS)
        dst_proj = share(at_proj, n_proj).rearrange("p (s t d) -> p s t d", s=SLOTS, t=TILES)
        scores = share(at_scores, EDGES)
        weights = share(at_scores + EDGES, EDGES)
        rows10 = share(0, GROUP * R_ATT * 2 * D).rearrange("p (k r d) -> p k r d", k=GROUP, r=R_ATT)
        rows8 = share(0, GROUP * R_GRU * PARTS * D // 2).bitcast(bf16)\
            .rearrange("p (k r q d) -> p k r q d", k=GROUP, r=R_GRU, q=PARTS)
        n_rows8 = GROUP * R_GRU * PARTS * D // 2
        src_idx8 = share(n_rows8, IDX).bitcast(i32)
        dst_window = share(n_rows8 + IDX, IDX).bitcast(i32)
        parts = share(0, W * PARTS * D // 2).bitcast(bf16).rearrange("p (w q d) -> p w q d", w=W, q=PARTS)
        onehot = sb("onehot", [P, TILES, P], bf16)
        att = sb("att", [P, 2, TILES])
        rescale_kept = sb("rescale_kept", [P, 1])
        node_max = sb("node_max", [P, W])
        step_max = sb("step_max", [P, 1])
        new_max = sb("new_max", [P, 1])
        neg_max = sb("neg_max", [P, 1])
        rescale = sb("rescale", [P, 1])
        stat = sb("stat", [P, W])
        stat2 = sb("stat2", [P, W])
        inv_sqrt_deg = sb("inv_sqrt_deg", [P, W])
        inv_deg = sb("inv_deg", [P, W])
        cat = sb("cat", [P, GROUP, 2 * D])
        cat_t = share(0, 2 * GROUP * P).rearrange("p (k c) -> p k c", k=2)
        gates = sb("gates", [P, GROUP, 4 * D])
        src_window = gates[:, :, :].rearrange("p g c -> p (g c)")[:, 0:IDX].bitcast(i32)
        hid = sb("hid", [P, GROUP, D])
        hid2 = sb("hid2", [P, GROUP, D])
        chunk_dst = acc[:, :, :].rearrange("p w d -> p (w d)")[0:ROUNDS, 0:SLOTS * EDGES].bitcast(i32)\
            .rearrange("p (c e) -> p c e", c=SLOTS)
        bounds = sb("bounds", [ROUNDS, 2 * SLOTS], i32)
        bounds_row = sb("bounds_row", [1, ROUNDS * 2 * SLOTS], i32)
        lanes_i = sb("lanes_i", [P, P], i32)
        lanes = sb("lanes", [P, P])
        ids_i = sb("ids_i", [P, 2, W], i32)
        window_start = sb("window_start", [P, W])
        node_id = sb("node_id", [P, W])
        ident = sb("ident", [P, P])
        w1_sb = sb("w1_sb", [2 * D, D])
        w2_sb = sb("w2_sb", [2 * D, D])
        w8_sb = sb("w8_sb", [D, R_GRU * D])
        w10_sb = sb("w10_sb", [D, R_ATT * D])
        wg_sb = sb("wg_sb", [2 * D, 4 * D])
        wr_sb = sb("wr_sb", [2 * D, 2 * D])
        b1_sb = sb("b1_sb", [P, D])
        b2_sb = sb("b2_sb", [P, D])
        bg_sb = sb("bg_sb", [P, 4 * D])
        bh_sb = hid2[:, 0:3, :].rearrange("p g d -> p (g d)")

        turned_ps = pb("turned_ps", [P, 1024])
        prod_ps = pb("prod_ps", [P, 2048])
        sums_ps = pb("sums_ps", [P, D + 1])

        N_CONST = 14
        const_loaded = sem("const_loaded")
        x_loaded = sem("x_loaded")
        iota_done = sem("iota_done")
        bounds_found = sem("bounds_found")
        bounds_saved = sem("bounds_saved")
        bounds_loaded = sem("bounds_loaded")
        dst_loaded = sem("dst_loaded")
        types_loaded = sem("types_loaded")
        normalised = sem("normalised")
        idx_ready = sem("idx_ready")
        windows_found = sem("windows_found")
        IDX_STEPS = (3, 3 + 3 + 2, 3 + 3 + 2 + 2 * 2 + 1)
        var_ready = sem("var_ready")
        std_ready = sem("std_ready")
        groups_done = sem("groups_done")
        out_written = sem("out_written")
        dve_done = sem("dve_done")
        apart = {e: sem(f"apart_{e}") for e in ("pool", "act", "dve", "pe")}

        def stand_alone(engine, name):
            engine.sem_inc(apart[name], 1)

        class Chain:

            def __init__(self, eng):
                self.eng, self.base, self.n = eng, 0, 0

            def link(self, ins):
                self.n += 1
                ins.then_inc(dve_done, 1)
                self.eng.wait_ge(dve_done, self.base + self.n)

        def stage(name, names):
            return {n: sem(f"{name}_{n}") for n in names}

        SLOT = [f"{a}{k}" for a in ("gathered", "ring_free") for k in range(SLOTS)]
        PASS = ["table_ready", "written", "staged", "onehot_ready", "sums_ready", "acc_added"]
        NODE = ["cat_ready", "turned", "copied", "multiplied", "taken"]
        TABLE = ["picked", "turned", "copied", "projected", "written0", "written1"]
        plain_slots = stage("plain", SLOT)
        passes = [{"before": n * ROUNDS, **plain_slots, **stage(f"pass{n}", PASS if n < 5 else PASS[2:])}
                  for n in range(6)]
        sages = [stage(f"sage{n}", NODE) for n in range(2)]
        gru = stage("gru", NODE + ["squashed", "new_ready", "cand_ready"])
        final = stage("final", NODE)
        tab8 = stage("tab8", TABLE + ["high", "rest", "mid", "low"])
        messages_summed = sem("messages_summed")
        centred, squared = sem("centred"), sem("squared")
        split = {a: sem(f"split_{a}") for a in ("made", "high", "rest", "mid")}
        tab10 = stage("tab10", TABLE + ["half0", "half1"])
        attn = stage("attn", SLOT + [f"{a}{k}" for a in ("attr_loaded", "dst_loaded") for k in range(SLOTS)] +
                     ["staged", "summed", "squashed", "scaled", "score_ready", "spread", "far_ready", "masked",
                      "max_ready", "neg_ready", "kept", "rescaled", "exp_ready", "turned", "copied", "sums_ready",
                      "acc_added"])

        def projected(k, R):
            return prod_ps[:, 2 * k * 512:2 * (k + 1) * 512].rearrange("p (b c) -> p b c", b=2)[:, :, 0:R * D // 2]\
                .rearrange("p b (r d) -> p b r d", d=D)

        def remainders(k):
            return (gates[:, :, :].rearrange("p g c -> p (g c)")[:, k * R_GRU * D:(k + 1) * R_GRU * D]
                    .rearrange("p (r d) -> p r d", d=D))

        block = ctx.enter_context(nc.Block())

        by_window = table.rearrange("(p w) (q d) -> p w q d", p=P, q=PARTS)
        HW = W // 2

        def load_bounds(eng, regs, i):
            eng.load(regs, bounds_row[0:1, bass.ds(i * 2 * SLOTS, 2 * SLOTS)])

        def windows(eng, regs, k):
            return eng.Fori(eng.snap(regs[2 * k], min_val=0, max_val=W - 1),
                            eng.snap(regs[2 * k + 1], min_val=1, max_val=W))

        def rounds(eng, one):
            with eng.Fori(0, ROUNDS - 1) as i:
                one(i, False)
            one(ROUNDS - 1, True)


        class Banks:

            def __init__(self, cols):
                self.cols, self.per_bank = cols, 512 // cols
                self.count = -(-GROUP // self.per_bank)
                self.buffers = 2 if self.count <= 2 else 1
                self.ahead = self.count * self.buffers

            def windows(self, q):
                return range(q * self.per_bank, min(GROUP, (q + 1) * self.per_bank))

            def bank(self, k, q):
                ws = self.windows(q)
                c = ((k % self.buffers) * self.count + q) * 512
                return prod_ps[:, c:c + len(ws) * self.cols].rearrange("p (w c) -> p w c", c=self.cols)

        def batches(one):
            def run(eng):
                with eng.Fori(0, B - 1) as i:
                    one(i, False)
                one(B - 1, True)
            return run

        batch_windows = [slice(b * BATCH, (b + 1) * BATCH) for b in range(B)]

        PIECES = ((0, 3), (3, GROUP))
        AHEAD = 2

        def piece(k):
            return {start: p for p, (start, end) in enumerate(PIECES)}.get(k)

        def of_batch(i, g=None):
            return [(j, BATCH * i + j) for j in
                    (range(BATCH) if g is None else range(GROUP * g, GROUP * (g + 1)))]

        def table_cat_t(g):
            return acc[0:D, :, :].rearrange("p w d -> p (w d)")[:, g * GROUP * P:(g + 1) * GROUP * P]

        @block.sync
        def _(sp):
            sp.dma_start(x_sb[:, :, :], x).then_inc(x_loaded, 16)
            sp.dma_start(chunk_dst, dst_rows).then_inc(dst_loaded, 16)
            sp.dma_start(dst_idx[:, :], dst).then_inc(const_loaded, 16)
            sp.dma_start(src_idx[:, :], src).then_inc(const_loaded, 16)
            for to, of in ((ident, identity), (w1_sb, w_sage1), (w2_sb, w_sage2), (w8_sb, w_types8),
                           (w10_sb, w_types10), (wg_sb, w_gru), (wr_sb, w_res)):
                sp.dma_start(to[:, :], of).then_inc(const_loaded, 16)
            for to, of in ((b1_sb[:, :], b_sage1), (b2_sb[:, :], b_sage2), (bg_sb[:, 0:3 * D], b_ih),
                           (bh_sb, b_hh), (bg_sb[:, 3 * D:4 * D], b_hh[:, 2 * D:3 * D])):
                sp.dma_start(to, of.to_broadcast([P, of.shape[1]])).then_inc(const_loaded, 16)

            def write_parts(n):
                with sp.Fori(0, B) as i:
                    at = bass.ds(BATCH * i, BATCH)
                    sp.wait_ge(passes[n]["table_ready"], i + 1)
                    sp.dma_start(by_window[:, at, :, :], parts[:, at, :, :]).then_inc(passes[n]["written"], 16)

            write_parts(0)
            sp.wait_ge(bounds_found, 1)
            sp.dma_start(bounds_dram, bounds[:, :]).then_inc(bounds_saved, 16)
            sp.wait_ge(bounds_saved, 16)
            sp.dma_start(bounds_row[:, :], bounds_dram.rearrange("(o i) b -> o (i b)", o=1))\
              .then_inc(bounds_loaded, 16)

            for n in range(1, 5):
                write_parts(n)

            def write_table(s, to, R, made, buffer):
                rows_of = to.rearrange("(p w r) d -> p w (r d)", p=P, r=R)
                for p in range(len(PIECES)):
                    sp.sem_inc(s[f"written{p}"], 16)
                with sp.Fori(0, NG) as g:
                    for p, (start, end) in enumerate(PIECES):
                        for by in made:
                            sp.wait_ge(s[by], AHEAD + GROUP * g + end)
                        sp.dma_start(rows_of[:, bass.ds(GROUP * g + start, end - start), :], buffer[:, start:end, :])\
                          .then_inc(s[f"written{p}"], 16)

            sp.wait_ge(normalised, B)
            sp.dma_start(type_idx, type8).then_inc(types_loaded, 16)
            write_table(tab8, table8, R_GRU, ["low"], rows8.rearrange("p k r q d -> p k (r q d)"))
            sp.wait_ge(normalised, 2 * B)
            sp.dma_start(type_idx, type10).then_inc(types_loaded, 16)
            write_table(tab10, table10, R_ATT, ["half0", "half1"], rows10.rearrange("p k r d -> p k (r d)"))
            for p in range(len(PIECES)):
                sp.wait_ge(tab10[f"written{p}"], 16 * (NG + 1))

            def attention_inputs(i, k, first):
                if not first:
                    sp.wait_ge(attn[f"ring_free{k}"], i)
                sp.dma_start(attr[:, k, :, :],
                             edge_attr[bass.ds(SLOTS * i + k, 1), :, :, :].rearrange("o p t d -> (o p) t d"))\
                  .then_inc(attn[f"attr_loaded{k}"], 16)
                sp.dma_start(dst_wide[:, k, :],
                             dst_rows[bass.ds(i, 1), k, :].to_broadcast([P, EDGES]))\
                  .then_inc(attn[f"dst_loaded{k}"], 16)

            for k in range(SLOTS):
                attention_inputs(0, k, True)
            with sp.Fori(1, ROUNDS) as i:
                for k in range(SLOTS):
                    attention_inputs(i, k, False)

            with sp.Fori(0, B) as i:
                sp.wait_ge(groups_done, 2 * i + 2)
                sp.dma_start(out[:, bass.ds(BATCH * i, BATCH), :],
                             x_sb[:, bass.ds(BATCH * i, BATCH), :]).then_inc(out_written, 16)
            sp.wait_ge(out_written, 16 * B)

        @block.gpsimd
        def _(pool):
            pool.iota(lanes_i[:, :], pattern=[[1, P]], base=0, channel_multiplier=0).then_inc(iota_done, 1)
            pool.iota(ids_i[:, 0, :], pattern=[[P, W]], base=0, channel_multiplier=0).then_inc(iota_done, 1)
            pool.iota(ids_i[:, 1, :], pattern=[[P, W]], base=0, channel_multiplier=1).then_inc(iota_done, 1)
            pool.memset(rows[:, :, :, 2 * D:ROW], 1.0).then_inc(iota_done, 1)
            pool.memset(part_rows[:, :, :, PARTS * D:PARTS * D + 1], 1.0).then_inc(iota_done, 1)

            def gather(k, t, from_, idx, to, s):
                pool.indirect_dma_start(out=to, out_offset=None, in_=from_,
                                        in_offset=bass.IndirectOffsetOnAxis(ap=idx[:, k, t:t + 1], axis=0))\
                    .then_inc(s[f"gathered{k}"], 16)

            def gather_pass(s, chunk):
                for k in range(SLOTS):
                    pool.wait_ge(s["staged"], k + 1)
                    chunk(k)
                with pool.Fori(1, ROUNDS) as i:
                    for k in range(SLOTS):
                        pool.wait_ge(s["staged"], SLOTS * i + k + 1)
                        pool.wait_ge(s[f"ring_free{k}"], s.get("before", 0) + i)
                        stand_alone(pool, "pool")
                        chunk(k)

            def plain_pass(s, from_):
                def chunk(k):
                    for t in range(TILES):
                        gather(k, t, from_, staged_src, part_rows[:, k, t, 0:PARTS * D], s)
                gather_pass(s, chunk)

            done = [0]

            def chained(ins):
                ins.then_inc(idx_ready, 1)
                done[0] += 1
                pool.wait_ge(idx_ready, done[0])

            def node_rows(idx, idx_window):
                chained(pool.tensor_scalar(idx[:, :], idx[:, :], float(W), None, ALU.mult))
                chained(pool.tensor_scalar(idx_window, idx_window, float(1 - P * W), None, ALU.mult))
                chained(pool.tensor_tensor(idx[:, :], idx[:, :], idx_window, ALU.add))

            def table_rows(to, idx, R):
                chained(pool.tensor_scalar(to, idx[:, :], float(R), None, ALU.mult))
                chained(pool.tensor_tensor(to, to, type_idx, ALU.add))

            pool.wait_ge(windows_found, 1)
            node_rows(src_idx, src_window)
            for n in range(5):
                pool.wait_ge(passes[n]["written"], 16 * B)
                plain_pass(passes[n], table)

            pool.wait_ge(windows_found, 2)
            node_rows(dst_idx, dst_window)
            pool.wait_ge(types_loaded, 16)
            table_rows(src_idx8, src_idx, R_GRU)
            for p in range(len(PIECES)):
                pool.wait_ge(tab8[f"written{p}"], 16 * (NG + 1))
            plain_pass(passes[5], table8)

            pool.wait_ge(types_loaded, 16 * 2)
            for idx in (src_idx, dst_idx):
                table_rows(idx[:, :], idx, R_ATT)
            chained(pool.tensor_scalar(dst_idx[:, :], dst_idx[:, :], 2.0, None, ALU.mult))
            assert done[0] == IDX_STEPS[2]
            for p in range(len(PIECES)):
                pool.wait_ge(tab10[f"written{p}"], 16 * (NG + 1))
            halves = table10.rearrange("n (b d) -> (n b) d", b=2)

            def attention_chunk(k):
                for t in range(TILES):
                    gather(k, t, table10, staged_src, rows[:, k, t, 0:2 * D], attn)
                    gather(k, t, halves, staged_dst, dst_proj[:, k, t, :], attn)
            gather_pass(attn, attention_chunk)

        @block.scalar
        def _(act):
            def stage_indices(s, m, k, pairs):
                for to, of in pairs:
                    last = act.activation(to[:, k, :], of[:, bass.ds(m * TILES, TILES)], ACT.Copy)
                last.then_inc(s["staged"], 1)

            def plain_pass(s, idx=src_idx):
                pairs = [(staged_src, idx)]
                for k in range(SLOTS):
                    stage_indices(s, k, k, pairs)
                with act.Fori(0, ROUNDS) as i:
                    for k in range(SLOTS):
                        act.wait_ge(s[f"gathered{k}"], 16 * TILES * (s["before"] + i + 1))
                        stand_alone(act, "act")
                        stage_indices(s, SLOTS * (i + 1) + k, k, pairs)
                act.wait_ge(s["staged"], SLOTS * (ROUNDS + 1))

            def copy_turned(s, banks, g, k):
                act.wait_ge(s["turned"], g + 1)
                act.wait_ge(s["multiplied"], banks.count * g)
                act.activation(cat_t[:, k, :], turned_ps[:, 0:GROUP * P], ACT.Copy).then_inc(s["copied"], 1)

            def node_stage(s, cols, finish=None, fill=None):
                banks = Banks(cols)

                def one(i, last):
                    for k in range(2):
                        if not (last and k == 1):
                            copy_turned(s, banks, 2 * i + k + 1, 1 - k)
                        if fill and not last:
                            fill(2 * i + k + 2)
                        if finish:
                            finish(2 * i + k)
                act.wait_ge(s["turned"], 1)
                act.activation(cat_t[:, 0, :], turned_ps[:, 0:GROUP * P], ACT.Copy).then_inc(s["copied"], 1)
                if fill:
                    fill(1)
                batches(one)(act)

            def pick(s, g, batches_ready):
                act.wait_ge(normalised, batches_ready)
                stand_alone(act, "act")
                act.activation(cat[:, :, 0:D], h_sb[:, bass.ds(GROUP * g, GROUP), :], ACT.Copy)\
                   .then_inc(s["picked"], 1)

            def copy_group(s, g, parity):
                act.wait_ge(s["turned"], g + 1)
                act.activation(table_cat_t(parity), turned_ps[0:D, 0:GROUP * P], ACT.Copy).then_inc(s["copied"], 1)

            def table_stage(s, before, take, end=None):
                def one(i, last):
                    for g in range(2):
                        if not (last and g == 1):
                            copy_group(s, 2 * i + g + 1, (g + 1) % 2)
                        if not last:
                            pick(s, 2 * i + g + 2, before + i + 2)
                        for j, u in of_batch(i, g):
                            p = piece(j % GROUP)
                            if p is not None:
                                act.wait_ge(s[f"written{p}"], 16 * (2 * i + g + 1))
                                stand_alone(act, "act")
                            take(j, u)
                    if end:
                        end(*of_batch(i)[-1])
                pick(s, 0, before + 1)
                copy_group(s, 0, 0)
                pick(s, 1, before + 1)
                batches(one)(act)

            def tab8_mid(j, u):
                act.wait_ge(tab8["rest"], AHEAD + u + 1)
                act.activation(rows8[:, j % GROUP, :, 1, :], remainders(j % 2), ACT.Copy).then_inc(tab8["mid"], 1)

            def tab8_take(j, u):
                act.wait_ge(tab8["projected"], u + 1)
                act.activation(rows8[:, j % GROUP, :, 0, :].rearrange("p (b r) d -> p b r d", b=2),
                               projected(j % 2, R_GRU), ACT.Copy).then_inc(tab8["high"], 1)
                if j:
                    tab8_mid(j - 1, u - 1)

            def tab10_take(j, u):
                act.activation(rows10[:, j % GROUP, R_ATT // 2:, D:2 * D],
                               h_sb[:, bass.ds(u, 1), :].to_broadcast([P, R_ATT // 2, D]), ACT.Copy)
                act.wait_ge(tab10["projected"], u + 1)
                act.activation(rows10[:, j % GROUP, R_ATT // 2:, 0:D], projected(j % 2, R_ATT)[:, 1, :, :], ACT.Copy)\
                   .then_inc(tab10["half1"], 1)

            def norm(n):
                for b in range(2):
                    act.wait_ge(centred, 2 * n + b + 1)
                    at = slice(b * HW, (b + 1) * HW)
                    act.activation(h_sb[:, at, :], y_sb[:, at, :], ACT.Square).then_inc(squared, 1)

            def root(n):
                act.wait_ge(var_ready, n)
                act.activation(stat2[:, :], stat[:, :], ACT.Sqrt).then_inc(std_ready, 1)

            def split_parts(n, v, rest):
                for b in range(B + 1):
                    if b < B:
                        act.wait_ge(split["made"], B * n + b + 1)
                        act.activation(parts[:, batch_windows[b], 0, :], v[:, batch_windows[b], :], ACT.Copy)\
                           .then_inc(split["high"], 1)
                    if b:
                        act.wait_ge(split["rest"], B * n + b)
                        at = batch_windows[b - 1]
                        act.activation(parts[:, at, 1, :], rest[:, at, :], ACT.Copy)\
                           .then_inc(split["mid"], 1)

            norm(0)
            root(1)
            split_parts(0, h_sb, y_sb)
            act.wait_ge(idx_ready, IDX_STEPS[0])
            plain_pass(passes[0])
            node_stage(sages[0], D)
            split_parts(1, h_sb, y_sb)
            plain_pass(passes[1])
            node_stage(sages[1], D)
            norm(1)
            root(2)
            root(3)
            for n in (2, 3, 4):
                split_parts(n, y_sb, y_sb)
                plain_pass(passes[n])
            norm(2)
            root(4)
            table_stage(tab8, 0, tab8_take, tab8_mid)
            act.wait_ge(idx_ready, IDX_STEPS[1])
            plain_pass(passes[5], src_idx8)

            def gru_gates(g):
                banks = Banks(4 * D)
                act.wait_ge(gru["taken"], banks.count * (g + 1) + banks.ahead)
                act.activation(gates[:, :, 0:2 * D], gates[:, :, 0:2 * D], ACT.Tanh, scale=0.5)\
                   .then_inc(gru["squashed"], 1)
                act.wait_ge(gru["cand_ready"], g + 1)
                act.activation(hid[:, :, :], hid[:, :, :], ACT.Tanh).then_inc(gru["new_ready"], 1)

            def gru_fill(g):
                act.activation(cat[:, :, 0:D], acc[:, bass.ds(g * GROUP, GROUP), 0:D], ACT.Copy)
                act.activation(cat[:, :, D:2 * D], h_sb[:, bass.ds(g * GROUP, GROUP), :], ACT.Copy)\
                   .then_inc(gru["cat_ready"], 1)

            act.wait_ge(messages_summed, 1)
            gru_fill(0)
            node_stage(gru, 4 * D, gru_gates, gru_fill)
            norm(3)
            root(5)
            table_stage(tab10, B, tab10_take)
            act.wait_ge(idx_ready, IDX_STEPS[2])

            pairs = [(staged_src, src_idx), (staged_dst, dst_idx)]
            for k in range(SLOTS):
                stage_indices(attn, k, k, pairs)
            bound = [act.alloc_register(f"act_bound{k}") for k in range(2 * SLOTS)]
            steps = act.alloc_register("act_steps")
            act.reg_mov(steps, 0)

            def prepare(i, k, m):
                act.wait_ge(attn[f"gathered{k}"], 2 * 16 * TILES * (i + 1))
                stand_alone(act, "act")
                stage_indices(attn, m + SLOTS, k, pairs)
                act.wait_ge(attn["summed"], m + 1)
                act.activation(dst_proj[:, k, :, :], dst_proj[:, k, :, :], ACT.Tanh).then_inc(attn["squashed"], 1)

            def attention_round(i, last):
                load_bounds(act, bound, i)
                for k in range(SLOTS):
                    if not (last and k == SLOTS - 1):
                        prepare(i + (k + 1) // SLOTS, (k + 1) % SLOTS, SLOTS * i + k + 1)
                    with windows(act, bound, k) as n:
                        s = act.snap(steps)
                        act.wait_ge(attn["neg_ready"], s + 1)
                        stand_alone(act, "act")
                        act.activation(rescale[:, :], node_max[:, bass.ds(n, 1)], ACT.Exp, bias=neg_max[:, 0:1])\
                           .then_inc(attn["rescaled"], 1)
                        for h in range(2):
                            part = scores[:, h * HALF * P:(h + 1) * HALF * P]
                            act.activation(part, part, ACT.Exp, bias=neg_max[:, 0:1]).then_inc(attn["exp_ready"], 1)
                            if h == 0:
                                act.wait_ge(attn["rescaled"], s + 1)
                                stand_alone(act, "act")
                                act.activation(node_max[:, bass.ds(n, 1)], new_max[:, :], ACT.Copy)
                        for h in range(2):
                            act.wait_ge(attn["turned"], 2 * s + h + 2)
                            act.activation(weights[:, h * HALF * P:(h + 1) * HALF * P],
                                           turned_ps[:, h * HALF * P:(h + 1) * HALF * P], ACT.Copy)\
                               .then_inc(attn["copied"], 1)
                        act.reg_add(steps, steps, 1)
            prepare(0, 0, 0)
            rounds(act, attention_round)
            node_stage(final, 2 * D)

        @block.tensor
        def _(pe):
            pe.wait_ge(const_loaded, 16 * N_CONST)
            pe.wait_ge(iota_done, 5)
            pe.wait_ge(bounds_loaded, 16)
            bound = [pe.alloc_register(f"pe_bound{k}") for k in range(2 * SLOTS)]
            steps = pe.alloc_register("pe_steps")

            def plain_pass(s):
                pe.reg_mov(steps, 0)
                with pe.Fori(0, ROUNDS) as i:
                    load_bounds(pe, bound, i)
                    for k in range(SLOTS):
                        pe.wait_ge(s[f"gathered{k}"], 16 * TILES * (s["before"] + i + 1))
                        stand_alone(pe, "pe")
                        with windows(pe, bound, k) as _n:
                            st = pe.snap(steps)
                            for t in range(TILES):
                                if t % HALF == 0:
                                    pe.wait_ge(s["onehot_ready"], 2 * st + t // HALF + 1)
                                for q in (2, 1, 0):
                                    n = D + 1 if q == 2 else D
                                    last = pe.matmul(sums_ps[:, 0:n], onehot[:, t, :],
                                                     part_rows[:, k, t, q * D:q * D + n],
                                                     start=(t == 0 and q == 2), stop=(t == TILES - 1 and q == 0))
                            last.then_inc(s["sums_ready"], 1)
                            pe.reg_add(steps, steps, 1)
                        pe.drain().then_inc(s[f"ring_free{k}"], 1)

            def turn(s, g):
                pe.wait_ge(s["cat_ready"], g + 1)
                for k in range(GROUP):
                    last = pe.transpose(turned_ps[:, k * P:(k + 1) * P], cat[:, k, :], ident[:, :])
                last.then_inc(s["turned"], 1)

            def node_stage(s, w, cols):
                banks = Banks(cols)

                def one(i, last_batch):
                    for k in range(2):
                        g = 2 * i + k
                        pe.wait_ge(s["copied"], g + 1)
                        if not (last_batch and k == 1):
                            turn(s, g + 1)
                        for q in range(banks.count):
                            pe.wait_ge(s["taken"], banks.count * g + q + 1)
                            for w_at, n in enumerate(banks.windows(q)):
                                last = pe.matmul(banks.bank(k, q)[:, w_at, :], cat_t[:, k, n * P:(n + 1) * P],
                                                 w[:, :], start=True, stop=True)
                            last.then_inc(s["multiplied"], 1)
                pe.sem_inc(s["multiplied"], banks.count)
                turn(s, 0)
                batches(one)(pe)

            def make_table(s, w, R, taken):
                half = R * D // 2

                def turn_group(g):
                    pe.wait_ge(s["picked"], g + 1)
                    stand_alone(pe, "pe")
                    for k in range(GROUP):
                        last = pe.transpose(turned_ps[0:D, k * P:(k + 1) * P], cat[:, k, 0:D], ident[:, :])
                    last.then_inc(s["turned"], 1)

                def one(i, last_batch):
                    for g in range(2):
                        pe.wait_ge(s["copied"], 2 * i + g + 1)
                        if not (last_batch and g == 1):
                            turn_group(2 * i + g + 1)
                        for j, u in of_batch(i, g):
                            for by in taken:
                                pe.wait_ge(s[by], u + 1)
                            k = j % GROUP
                            for h in range(2):
                                c = (2 * (j % 2) + h) * 512
                                last = pe.matmul(prod_ps[:, c:c + half], table_cat_t(g)[:, k * P:(k + 1) * P],
                                                 w[:, h * half:(h + 1) * half], start=True, stop=True)
                            last.then_inc(s["projected"], 1)
                turn_group(0)
                batches(one)(pe)

            plain_pass(passes[0])
            node_stage(sages[0], w1_sb, D)
            plain_pass(passes[1])
            node_stage(sages[1], w2_sb, D)
            for n in (2, 3, 4):
                plain_pass(passes[n])
            make_table(tab8, w8_sb, R_GRU, ["rest"])
            plain_pass(passes[5])
            node_stage(gru, wg_sb, 4 * D)
            make_table(tab10, w10_sb, R_ATT, ["half0", "half1"])

            pe.reg_mov(steps, 0)

            def spread(m, k):
                pe.wait_ge(attn["score_ready"], m + 1)
                for t in range(TILES):
                    c = (k % 2) * EDGES + t * P
                    last = pe.matmul(prod_ps[:, c:c + P], att[:, k % 2, t:t + 1].to_broadcast([P, P]),
                                     ident[:, :], start=True, stop=True)
                last.then_inc(attn["spread"], 1)

            def attention_round(i, last_round):
                load_bounds(pe, bound, i)
                for k in range(SLOTS):
                    if not (last_round and k == SLOTS - 1):
                        spread(SLOTS * i + k + 1, k + 1)
                    with windows(pe, bound, k) as _n:
                        st = pe.snap(steps)
                        for h in range(2):
                            pe.wait_ge(attn["exp_ready"], 2 * st + h + 1)
                            for t in range(h * HALF, (h + 1) * HALF):
                                last = pe.transpose(turned_ps[:, t * P:(t + 1) * P], scores[:, t * P:(t + 1) * P],
                                                    ident[:, :])
                            last.then_inc(attn["turned"], 1)
                        pe.wait_ge(attn["acc_added"], st + 2)
                        for t in range(TILES):
                            if t % HALF == 0:
                                pe.wait_ge(attn["copied"], 2 * st + t // HALF + 1)
                            last = pe.matmul(sums_ps[:, :], weights[:, t * P:(t + 1) * P], rows[:, k, t, D:ROW],
                                             start=(t == 0), stop=(t == TILES - 1))
                        last.then_inc(attn["sums_ready"], 1)
                        pe.reg_add(steps, steps, 1)
                    pe.drain().then_inc(attn[f"ring_free{k}"], 1)
            pe.sem_inc(attn["turned"], 1)
            pe.sem_inc(attn["sums_ready"], 1)
            spread(0, 0)
            rounds(pe, attention_round)
            node_stage(final, wr_sb, 2 * D)

        @block.vector
        def _(dve):
            chain = Chain(dve)
            link = chain.link
            bound = [dve.alloc_register(f"dve_bound{k}") for k in range(2 * SLOTS)]
            steps = dve.alloc_register("dve_steps")
            last_window = dve.alloc_register("dve_last_window")

            def per_node(v):
                return v.unsqueeze(2).to_broadcast([P, v.shape[1], D])

            def layer_norm(n):
                link(dve.tensor_reduce(stat[:, :], x_sb[:, :, :], AX.X, ALU.add))
                link(dve.tensor_scalar(stat[:, :], stat[:, :], 1.0 / D, None, ALU.mult))
                for b in range(2):
                    at = slice(b * HW, (b + 1) * HW)
                    dve.tensor_tensor(y_sb[:, at, :], x_sb[:, at, :], per_node(stat[:, at]), ALU.subtract)\
                       .then_inc(centred, 1)
                dve.wait_ge(centred, 2 * norms[0] + 2)
                for b in range(2):
                    at = slice(b * HW, (b + 1) * HW)
                    dve.wait_ge(squared, 2 * norms[0] + b + 1)
                    link(dve.tensor_reduce(stat[:, at], h_sb[:, at, :], AX.X, ALU.add))
                norms[0] += 1
                dve.tensor_scalar(stat[:, :], stat[:, :], 1.0 / D, EPS, ALU.mult, ALU.add).then_inc(var_ready, 1)
                dve.wait_ge(std_ready, n)
                link(dve.reciprocal(stat[:, :], stat2[:, :]))
            norms = [0]

            def normalise_all():
                for at in batch_windows:
                    normalise(at).then_inc(normalised, 1)

            def normalise(at):
                return dve.scalar_tensor_tensor(h_sb[:, at, :], y_sb[:, at, :], 0.0, per_node(stat[:, at]),
                                                ALU.max, ALU.mult)

            def save_table(n, v, rest, make=None):
                if make is None:
                    dve.sem_inc(split["made"], B)
                for b in range(B + 2):
                    if b < B and make is not None:
                        make(batch_windows[b]).then_inc(split["made"], 1)
                    if 1 <= b <= B:
                        at = batch_windows[b - 1]
                        dve.wait_ge(split["high"], B * n + b)
                        dve.tensor_tensor(rest[:, at, :], v[:, at, :], parts[:, at, 0, :], ALU.subtract)\
                           .then_inc(split["rest"], 1)
                    if b >= 2:
                        at = batch_windows[b - 2]
                        dve.wait_ge(split["mid"], B * n + b - 1)
                        dve.tensor_tensor(parts[:, at, 2, :], rest[:, at, :], parts[:, at, 1, :], ALU.subtract)\
                           .then_inc(passes[n]["table_ready"], 1)

            def plain_pass(s):
                dve.memset(acc[:, :, :], 0.0).then_inc(s["acc_added"], 1)
                dve.reg_mov(steps, 0)
                with dve.Fori(0, ROUNDS) as i:
                    load_bounds(dve, bound, i)
                    for k in range(SLOTS):
                        with windows(dve, bound, k) as n:
                            st = dve.snap(steps)
                            dve.wait_ge(s["acc_added"], st + 1)
                            for h in range(2):
                                here = dst_f[:, bass.ds((SLOTS * i + k) * TILES + h * HALF, HALF)].unsqueeze(2)\
                                    .to_broadcast([P, HALF, P])
                                dve.scalar_tensor_tensor(onehot[:, h * HALF:(h + 1) * HALF, :], here,
                                                         window_start[:, bass.ds(n, 1)],
                                                         lanes[:, :].unsqueeze(1).to_broadcast([P, HALF, P]),
                                                         ALU.subtract, ALU.is_equal).then_inc(s["onehot_ready"], 1)
                            dve.wait_ge(s["sums_ready"], st + 1)
                            at = acc[:, bass.ds(n, 1), :].rearrange("p o d -> p (o d)")
                            dve.tensor_tensor(at, at, sums_ps[:, :], ALU.add).then_inc(s["acc_added"], 1)
                            dve.reg_add(steps, steps, 1)
                dve.wait_ge(s["acc_added"], dve.snap(steps) + 1)
                stand_alone(dve, "dve")

            def group(buf, g):
                return buf[:, bass.ds(g * GROUP, GROUP), 0:D]

            def node_stage(s, cols, fill, take, finish, links):
                banks = Banks(cols)

                def one(i, last):
                    for k in range(2):
                        g = 2 * i + k
                        if fill and not last:
                            dve.wait_ge(s["turned"], g + 2)
                            stand_alone(dve, "dve")
                            fill(g + 2)
                        for q in range(banks.count):
                            dve.wait_ge(s["multiplied"], banks.count * (g + 1) + q + 1)
                            ws = banks.windows(q)
                            take(slice(ws[0], ws[-1] + 1), banks.bank(k, q)).then_inc(s["taken"], 1)
                        dve.wait_ge(s["taken"], banks.count * (g + 1) + banks.ahead)
                        stand_alone(dve, "dve")
                        finish(g)
                dve.sem_inc(s["taken"], banks.ahead)
                if fill:
                    fill(0)
                    dve.wait_ge(s["turned"], 1)
                    fill(1)
                start = chain.n
                with dve.Fori(0, NG // 2 - 1) as i:
                    chain.base, chain.n = i * 2 * links + start, 0
                    one(i, False)
                    assert chain.n == 2 * links
                chain.base, chain.n = 0, start + (NG - 2) * links
                one(NG // 2 - 1, True)

            def find_windows(to, idx):
                dve.wait_ge(const_loaded, 16 * N_CONST)
                dve.tensor_scalar(to, idx[:, :], P.bit_length() - 1, None, ALU.arith_shift_right)\
                   .then_inc(windows_found, 1)

            dve.wait_ge(x_loaded, 16)
            layer_norm(1)
            find_windows(src_window, src_idx)
            save_table(0, h_sb, y_sb, normalise)
            dve.wait_ge(dst_loaded, 16)
            lohi = bounds[:, :].rearrange("p (c b) -> p c b", b=2)
            link(dve.tensor_reduce(lohi[:, :, 0], chunk_dst, AX.X, ALU.min))
            link(dve.tensor_reduce(lohi[:, :, 1], chunk_dst, AX.X, ALU.max))
            link(dve.tensor_scalar(bounds[:, :], bounds[:, :], 7, None, ALU.arith_shift_right))
            dve.tensor_scalar(lohi[:, :, 1], lohi[:, :, 1], 1.0, None, ALU.add).then_inc(bounds_found, 1)
            dve.wait_ge(iota_done, 5)
            link(dve.tensor_copy(lanes[:, :], lanes_i[:, :]))
            link(dve.tensor_copy(window_start[:, :], ids_i[:, 0, :]))
            link(dve.tensor_copy(node_id[:, :], ids_i[:, 1, :]))
            dve.wait_ge(const_loaded, 16 * N_CONST)
            link(dve.tensor_copy(dst_f[:, :], dst_idx[:, 0:chunks * TILES]))
            link(dve.tensor_tensor(bg_sb[:, 0:2 * D], bg_sb[:, 0:2 * D], bh_sb[:, 0:2 * D], ALU.add))
            dve.wait_ge(bounds_loaded, 16)

            def sage(s, bias, put):
                link(dve.tensor_scalar(stat[:, :], acc[:, :, D], 1.0, None, ALU.max))
                link(dve.reciprocal(stat2[:, :], stat[:, :]))

                def fill(g):
                    dve.tensor_tensor(cat[:, :, 0:D], group(acc, g),
                                      stat2[:, bass.ds(g * GROUP, GROUP)].unsqueeze(2)
                                      .to_broadcast([P, GROUP, D]), ALU.mult)
                    dve.tensor_copy(cat[:, :, D:2 * D], group(h_sb, g)).then_inc(s["cat_ready"], 1)

                def take(ws, products):
                    return dve.tensor_tensor(hid[:, ws, :], products,
                                             bias[:, :].unsqueeze(1).to_broadcast([P, GROUP, D]), ALU.add)
                node_stage(s, D, fill, take, lambda g: link(put(g)), 1)

            plain_pass(passes[0])
            sage(sages[0], b1_sb,
                 lambda g: dve.tensor_scalar(group(h_sb, g), hid[:, :, :], 0.0, None, ALU.max))
            save_table(1, h_sb, y_sb)
            plain_pass(passes[1])
            sage(sages[1], b2_sb,
                 lambda g: dve.scalar_tensor_tensor(group(x_sb, g), hid[:, :, :], 0.0, group(x_sb, g),
                                                    ALU.max, ALU.add))

            layer_norm(2)
            link(normalise(slice(0, W)))
            link(dve.tensor_scalar(inv_sqrt_deg[:, :], acc[:, :, D], 1.0, None, ALU.min))
            dve.tensor_scalar(stat[:, :], acc[:, :, D], 1.0, None, ALU.max).then_inc(var_ready, 1)
            dve.wait_ge(std_ready, 3)
            link(dve.reciprocal(stat[:, :], stat2[:, :]))
            link(dve.tensor_tensor(inv_sqrt_deg[:, :], inv_sqrt_deg[:, :], stat[:, :], ALU.mult))
            link(dve.tensor_tensor(inv_deg[:, :], inv_sqrt_deg[:, :], inv_sqrt_deg[:, :], ALU.mult))
            for n in (2, 3, 4):
                of, factor = (h_sb, inv_sqrt_deg) if n == 2 else (acc, inv_deg)
                save_table(n, y_sb, y_sb,
                           lambda at: dve.tensor_tensor(y_sb[:, at, :], of[:, at, 0:D], per_node(factor[:, at]),
                                                        ALU.mult))
                if n > 2:
                    link(dve.tensor_tensor(h_sb[:, :, :], acc[:, :, 0:D], per_node(inv_sqrt_deg[:, :]), ALU.mult))
                link(dve.scalar_tensor_tensor(x_sb[:, :, :], h_sb[:, :, :], 0.25, x_sb[:, :, :], ALU.mult, ALU.add))
                plain_pass(passes[n])
            link(dve.tensor_tensor(h_sb[:, :, :], acc[:, :, 0:D], per_node(inv_sqrt_deg[:, :]), ALU.mult))
            link(dve.scalar_tensor_tensor(x_sb[:, :, :], h_sb[:, :, :], 0.25, x_sb[:, :, :], ALU.mult, ALU.add))

            layer_norm(4)
            normalise_all()
            find_windows(dst_window, dst_idx)

            def tab8_low(j, u):
                dve.wait_ge(tab8["mid"], u + 1)
                dve.tensor_tensor(rows8[:, j % GROUP, :, 2, :], remainders(j % 2), rows8[:, j % GROUP, :, 1, :],
                                  ALU.subtract).then_inc(tab8["low"], 1)

            def tab8_batch(i, last):
                for j, u in of_batch(i):
                    dve.wait_ge(tab8["high"], u + 1)
                    dve.wait_ge(tab8["low"], u + 1)
                    dve.tensor_tensor(remainders(j % 2).rearrange("p (b r) d -> p b r d", b=2),
                                      projected(j % 2, R_GRU),
                                      rows8[:, j % GROUP, :, 0, :].rearrange("p (b r) d -> p b r d", b=2),
                                      ALU.subtract).then_inc(tab8["rest"], 1)
                    if j:
                        tab8_low(j - 1, u - 1)
                tab8_low(*of_batch(i)[-1])
            dve.sem_inc(tab8["rest"], AHEAD)
            dve.sem_inc(tab8["low"], AHEAD)
            batches(tab8_batch)(dve)
            plain_pass(passes[5])

            dve.sem_inc(messages_summed, 1)

            def gru_take(ws, products):
                n = ws.stop - ws.start
                return dve.tensor_tensor(gates[:, ws, :], products,
                                         bg_sb[:, :].unsqueeze(1).to_broadcast([P, n, 4 * D]), ALU.add)

            def gru_finish(g):
                dve.wait_ge(gru["squashed"], g + 1)
                link(dve.scalar_tensor_tensor(hid[:, :, :], gates[:, :, 0:D], 1.0, gates[:, :, 3 * D:4 * D],
                                              ALU.add, ALU.mult))
                dve.scalar_tensor_tensor(hid[:, :, :], hid[:, :, :], 0.5, gates[:, :, 2 * D:3 * D],
                                         ALU.mult, ALU.add).then_inc(gru["cand_ready"], 1)
                dve.wait_ge(gru["new_ready"], g + 1)
                link(dve.tensor_tensor(hid2[:, :, :], group(h_sb, g), hid[:, :, :], ALU.subtract))
                link(dve.scalar_tensor_tensor(hid2[:, :, :], gates[:, :, D:2 * D], 1.0, hid2[:, :, :],
                                              ALU.add, ALU.mult))
                link(dve.scalar_tensor_tensor(hid2[:, :, :], hid2[:, :, :], 0.5, hid[:, :, :], ALU.mult, ALU.add))
                link(dve.tensor_tensor(group(x_sb, g), group(x_sb, g), hid2[:, :, :], ALU.add))
            node_stage(gru, 4 * D, None, gru_take, gru_finish, 5)

            layer_norm(5)
            normalise_all()
            dve.wait_ge(normalised, 2 * B)

            def tab10_batch(i, last):
                for j, u in of_batch(i):
                    p = piece(j % GROUP)
                    if p is not None:
                        dve.wait_ge(tab10[f"written{p}"], 16 * (2 * i + j // GROUP + 1))
                        stand_alone(dve, "dve")
                    dve.tensor_copy(rows10[:, j % GROUP, 0:R_ATT // 2, D:2 * D],
                                    h_sb[:, bass.ds(u, 1), :].to_broadcast([P, R_ATT // 2, D]))
                    dve.wait_ge(tab10["projected"], u + 1)
                    dve.tensor_copy(rows10[:, j % GROUP, 0:R_ATT // 2, 0:D], projected(j % 2, R_ATT)[:, 0, :, :])\
                       .then_inc(tab10["half0"], 1)
            dve.sem_inc(tab10["half0"], AHEAD)
            dve.sem_inc(tab10["half1"], AHEAD)
            batches(tab10_batch)(dve)

            link(dve.memset(node_max[:, :], LOW))
            link(dve.memset(sums_ps[:, :], 0.0))
            link(dve.memset(rescale[:, :], 1.0))
            dve.memset(acc[:, :, :], 0.0).then_inc(attn["acc_added"], 1)
            dve.reg_mov(steps, 0)
            dve.reg_mov(last_window, 0)

            def prepare(i, k, m):
                proj = dst_proj[:, k, :, :]
                dve.wait_ge(attn[f"gathered{k}"], 2 * 16 * TILES * (i + 1))
                dve.wait_ge(attn[f"attr_loaded{k}"], 16 * (i + 1))
                dve.tensor_tensor(proj, proj, attr[:, k, :, :], ALU.add).then_inc(attn["summed"], 1)
                dve.wait_ge(attn["squashed"], m + 1)
                dve.tensor_tensor(proj, proj, rows[:, k, :, 0:D], ALU.mult).then_inc(attn["scaled"], 1)
                dve.wait_ge(attn["scaled"], m + 1)
                dve.tensor_reduce(att[:, k % 2, :], proj, AX.X, ALU.add).then_inc(attn["score_ready"], 1)

            def add_sums(count):
                dve.wait_ge(attn["sums_ready"], count)
                at = acc[:, bass.ds(dve.snap(last_window, min_val=0, max_val=W - 1), 1), :]\
                    .rearrange("p o d -> p (o d)")
                dve.scalar_tensor_tensor(at, at, rescale_kept[:, 0:1], sums_ps[:, :], ALU.mult, ALU.add)\
                   .then_inc(attn["acc_added"], 1)

            def attention_round(i, last):
                load_bounds(dve, bound, i)
                for k in range(SLOTS):
                    m = SLOTS * i + k
                    if not (last and k == SLOTS - 1):
                        prepare(i + (k + 1) // SLOTS, (k + 1) % SLOTS, m + 1)
                    dve.wait_ge(attn["spread"], m + 1)
                    dve.wait_ge(attn[f"dst_loaded{k}"], 16 * (i + 1))
                    stand_alone(dve, "dve")
                    with windows(dve, bound, k) as n:
                        st = dve.snap(steps)
                        dve.wait_ge(attn["turned"], 2 * st + 1)
                        stand_alone(dve, "dve")
                        dve.tensor_scalar(scores, dst_wide[:, k, :], node_id[:, bass.ds(n, 1)], FAR,
                                          ALU.not_equal, ALU.mult).then_inc(attn["far_ready"], 1)
                        dve.wait_ge(attn["acc_added"], st + 1)
                        stand_alone(dve, "dve")
                        dve.tensor_copy(rescale_kept[:, :], rescale[:, :]).then_inc(attn["kept"], 1)
                        dve.wait_ge(attn["far_ready"], st + 1)
                        stand_alone(dve, "dve")
                        c = (k % 2) * EDGES
                        dve.tensor_tensor_reduce(out=scores, in0=scores, in1=prod_ps[:, c:c + EDGES],
                                                 scale=1.0, scalar=FAR, op0=ALU.add, op1=ALU.max,
                                                 accum_out=step_max[:, :]).then_inc(attn["masked"], 1)
                        dve.wait_ge(attn["masked"], st + 1)
                        dve.tensor_tensor(new_max[:, :], step_max[:, :], node_max[:, bass.ds(n, 1)], ALU.max)\
                           .then_inc(attn["max_ready"], 1)
                        dve.wait_ge(attn["max_ready"], st + 1)
                        dve.tensor_scalar(neg_max[:, :], new_max[:, :], -1.0, None, ALU.mult)\
                           .then_inc(attn["neg_ready"], 1)
                        dve.wait_ge(attn["kept"], st + 1)
                        add_sums(st + 1)
                        dve.reg_mov(last_window, n)
                        dve.reg_add(steps, steps, 1)
            prepare(0, 0, 0)
            rounds(dve, attention_round)
            dve.wait_ge(attn["sums_ready"], dve.snap(steps) + 1)
            dve.wait_ge(attn["acc_added"], dve.snap(steps) + 1)
            stand_alone(dve, "dve")
            link(dve.tensor_copy(rescale_kept[:, :], rescale[:, :]))
            add_sums(dve.snap(steps) + 1)
            dve.wait_ge(attn["acc_added"], dve.snap(steps) + 2)
            stand_alone(dve, "dve")
            link(dve.tensor_scalar(stat[:, :], acc[:, :, D], 1.0e-30, None, ALU.max))
            link(dve.reciprocal(stat2[:, :], stat[:, :]))
            link(dve.tensor_tensor(y_sb[:, :, :], acc[:, :, 0:D], per_node(stat2[:, :]), ALU.mult))

            def final_fill(g):
                dve.tensor_tensor(cat[:, :, 0:D], group(y_sb, g), group(h_sb, g), ALU.add)
                dve.tensor_tensor(cat[:, :, D:2 * D], group(y_sb, g), group(h_sb, g), ALU.mult)\
                   .then_inc(final["cat_ready"], 1)

            def final_take(ws, products):
                return dve.tensor_copy(gates[:, ws, 0:2 * D], products)

            def final_finish(g):
                both = gates[:, :, 0:2 * D]
                link(dve.scalar_tensor_tensor(both, both, SLOPE, both, ALU.mult, ALU.max))
                link(dve.tensor_tensor(group(x_sb, g), group(x_sb, g), gates[:, :, 0:D], ALU.add))
                link(dve.tensor_tensor(group(x_sb, g), group(x_sb, g), gates[:, :, D:2 * D], ALU.add))
                dve.sem_inc(groups_done, 1)
            node_stage(final, 2 * D, final_fill, final_take, final_finish, 3)


def kernel(**inputs):
    import numpy as np
    import concourse.bacc as bacc
    from concourse.bass_utils import run_bass_kernel_spmd

    a = {k: np.asarray(v) for k, v in inputs.items()}
    n_nodes, n_edges = a["x"].shape[0], a["src"].shape[0]
    tile_group = P * GROUP * 2
    nodes = -(-n_nodes // tile_group) * tile_group
    edges = P * TILES
    rounds = -(-n_edges // (SLOTS * edges))
    padded = rounds * SLOTS * edges
    tiles = padded // P

    def edge_list(v, fill):
        e = np.full([padded], fill, v.dtype)
        e[:n_edges] = v
        cols = np.zeros([P, tiles + SLOTS * TILES], v.dtype)
        cols[:, :tiles] = e.reshape(tiles, P).T
        return e, cols

    x = np.zeros([nodes, D], a["x"].dtype)
    x[:n_nodes] = a["x"]
    x = np.ascontiguousarray(x.reshape(nodes // P, P, D).transpose(1, 0, 2))
    dst_flat, dst = edge_list(a["dst"], nodes - 1)
    attr = np.zeros([padded, D], a["edge_attr_64"].dtype)
    attr[:n_edges] = a["edge_attr_64"]
    T = lambda name: np.ascontiguousarray(a[name].T)
    w_ih, w_hh = T("L2_gnn_w_ih"), T("L2_gnn_w_hh")
    w_gru = np.zeros([2 * D, 4 * D], w_ih.dtype)
    w_gru[:D, :3 * D] = w_ih
    w_gru[D:, :2 * D] = w_hh[:, :2 * D]
    w_gru[D:, 3 * D:] = w_hh[:, 2 * D:]
    w_res = np.zeros([2 * D, 2 * D], w_ih.dtype)
    w_res[:D, :D] = T("L3_gnn_res_fc_w")
    w_res[D:, D:] = T("L3_gnn_res_fc2_w")
    arrays = {
        "x": x,
        "src": edge_list(a["src"], 0)[1],
        "dst": dst,
        "dst_rows": dst_flat.reshape(rounds, SLOTS, edges),
        "type8": edge_list(a["edge_type_8"], 0)[1],
        "type10": edge_list(a["edge_type_10"], 0)[1],
        "edge_attr": np.ascontiguousarray(attr.reshape(rounds * SLOTS, TILES, P, D).transpose(0, 2, 1, 3)),
        "w_sage1": np.concatenate([T("L0_gnn_W_l1"), T("L0_gnn_W_r1")]),
        "w_sage2": np.concatenate([T("L0_gnn_W_l2"), T("L0_gnn_W_r2")]),
        "b_sage1": a["L0_gnn_b1"][None, :],
        "b_sage2": a["L0_gnn_b2"][None, :],
        "w_types8": np.ascontiguousarray(a["L2_gnn_edge_matrix"].reshape(R_GRU, D, D).transpose(2, 0, 1)
                                         .reshape(D, R_GRU * D)),
        "w_gru": w_gru,
        "b_ih": a["L2_gnn_b_ih"][None, :],
        "b_hh": a["L2_gnn_b_hh"][None, :],
        "w_types10": np.ascontiguousarray(a["L3_gnn_relation_weight"].transpose(1, 0, 2).reshape(D, R_ATT * D)),
        "w_res": w_res,
        "identity": np.eye(P, dtype=np.float32),
    }
    nc = bacc.Bacc("TRN2", target_bir_lowering=False, num_devices=1)
    args = {n: nc.dram_tensor(f"in_{n}", v.shape, mybir.dt.from_np(v.dtype), kind="ExternalInput").ap()
            for n, v in arrays.items()}
    out = nc.dram_tensor("out", [P, nodes // P, D], mybir.dt.float32, kind="ExternalOutput").ap()
    build(nc, out=out, **args)
    r = run_bass_kernel_spmd(nc, [{f"in_{n}": v for n, v in arrays.items()}], core_ids=[0])
    return r.results[0]["out"].transpose(1, 0, 2).reshape(nodes, D)[:n_nodes]
```
